# Optimizing a Trainium2 kernel written in Bass

```python
import numpy as np
import jax
import jax.numpy as jnp

def _softmax(x, axis=-1):
    return jax.nn.softmax(x, axis=axis)

def _gelu(x):
    return jax.nn.gelu(x, approximate=True)

def _silu(x):
    return jax.nn.silu(x)

def _sigmoid(x):
    return jax.nn.sigmoid(x)

def _layernorm(x, axis=-1, eps=1e-05):
    m = jnp.mean(x, axis=axis, keepdims=True)
    v = jnp.var(x, axis=axis, keepdims=True)
    return (x - m) / jnp.sqrt(v + eps)

def _scatter_add(tgt, idx, src, axis=0):
    return tgt.at[idx].add(src)

def _segment_sum(src, seg, n):
    return jax.ops.segment_sum(src, seg, n)
kernel_name = 'mk_xattn_ffn_d1_seqx_r8_fab4b9'

def setup_inputs(seed: int=0):
    np.random.seed(seed)
    _w = jnp.asarray

    def _rec_inputs():
        import jax
        import jax.numpy as jnp
        _rk = jax.random.key(seed)
        x = -0.000125 + 0.9999 * jax.random.normal(jax.random.fold_in(_rk, 1), (32, 64, 512), jnp.float32)
        _lenS = 64 - jax.random.randint(jax.random.fold_in(_rk, 7), (32,), 0, max(1, 64 // 4) + 1, jnp.int32)
        _lenS2 = 64 - jax.random.randint(jax.random.fold_in(_rk, 8), (32,), 0, max(1, 64 // 4) + 1, jnp.int32)
        _ctx_4096P = jax.random.normal(jax.random.fold_in(_rk, 11), (32, 16, 512), jnp.float32)
        _ctx_4096c = jax.random.dirichlet(jax.random.fold_in(_rk, 511), 0.3 * jnp.ones((16,), jnp.float32), (32, 64))
        _ctx_4096t = jnp.einsum('bsk,bkd->bsd', _ctx_4096c, _ctx_4096P)
        _ctx_4096t = _ctx_4096t * jax.lax.rsqrt(jnp.mean(jnp.square(_ctx_4096t)) + 1e-12) * 0.953939
        ctx_4096 = -1.52775e-05 + 0.999936 * (_ctx_4096t + 0.3 * jax.random.normal(jax.random.fold_in(_rk, 611), (32, 64, 512), jnp.float32))
        return (x, ctx_4096)
    x, ctx_4096 = _rec_inputs()

    def _L0_xattn_setup():
        import jax, jax.numpy as jnp
        import numpy as np
        H = 8
        C = 2

        def _autocorrelation(Q, K, V):
            B, L, D = Q.shape
            d = D // H
            q = Q.reshape(B, L, H, d).transpose(0, 2, 1, 3)
            k = K.reshape(B, L, H, d).transpose(0, 2, 1, 3)
            v = V.reshape(B, L, H, d).transpose(0, 2, 1, 3)
            qf = jnp.fft.fft(q, axis=2)
            kf = jnp.fft.fft(k, axis=2)
            corr = jnp.fft.ifft(qf * jnp.conj(kf), axis=2).real
            topk = int(C * np.log(L))
            w, idx = jax.lax.top_k(corr.transpose(0, 1, 3, 2), topk)
            w = jax.nn.softmax(w, axis=-1)
            pos = jnp.arange(L)[:, None]
            out = jnp.zeros_like(v)
            for i in range(topk):
                g = jnp.minimum(idx[:, :, None, :, i] + pos, L - 1)
                out = out + w[:, :, None, :, i] * jnp.take_along_axis(v, g, axis=2)
            return out.transpose(0, 2, 1, 3).reshape(B, L, D)
        key = jax.random.key(seed)
        k1, k2, k3 = jax.random.split(key, 3)
        B, L, D = (16, 64, 512)
        Q = jax.random.normal(k1, (B, L, D), dtype=jnp.float32)
        K = jax.random.normal(k2, (B, L, D), dtype=jnp.float32)
        V = jax.random.normal(k3, (B, L, D), dtype=jnp.float32)
        return {'Q': Q, 'K': K, 'V': V}
    _L0_xattn_all = _L0_xattn_setup()
    _L0_xattn_in = {k: v for k, v in _L0_xattn_all.items() if k in ()}
    del _L0_xattn_all

    def _L0_ffn_setup():
        import jax, jax.numpy as jnp
        import numpy as np
        HIDDEN = 512
        MOE_INTER = 128
        SHARED_INTER = 512
        NUM_EXPERTS = 16
        TOP_K = 2

        def _moe_forward(x, gate_w, w_gate_up, w_down, shared_w_gate_up, shared_w_down):
            orig_shape = x.shape
            x2 = x.reshape(-1, orig_shape[-1])
            gu_s = x2 @ shared_w_gate_up.T
            g_s, u_s = jnp.split(gu_s, 2, axis=-1)
            shared_out = jax.nn.silu(g_s) * u_s @ shared_w_down.T
            logits = x2 @ gate_w.T
            probs = jax.nn.softmax(logits, axis=-1)
            topk_vals, topk_idx = jax.lax.top_k(probs, TOP_K)
            topk_vals = topk_vals / jnp.sum(topk_vals, axis=-1, keepdims=True)
            combine = jnp.sum(jax.nn.one_hot(topk_idx, NUM_EXPERTS, dtype=x2.dtype) * topk_vals[..., None], axis=1)
            gu = jnp.einsum('th,eih->eti', x2, w_gate_up)
            g, u = jnp.split(gu, 2, axis=-1)
            act = jax.nn.silu(g) * u
            out_e = jnp.einsum('eti,ehi->eth', act, w_down)
            moe_out = jnp.einsum('eth,te->th', out_e, combine)
            return (moe_out + shared_out).reshape(orig_shape)
        key = jax.random.key(seed)
        ks = jax.random.split(key, 6)
        s = 0.02
        hidden_states = jax.random.normal(ks[0], (2, 256, HIDDEN), dtype=jnp.float32)
        gate_w = jax.random.normal(ks[1], (NUM_EXPERTS, HIDDEN), dtype=jnp.float32) * s
        w_gate_up = jax.random.normal(ks[2], (NUM_EXPERTS, 2 * MOE_INTER, HIDDEN), dtype=jnp.float32) * s
        w_down = jax.random.normal(ks[3], (NUM_EXPERTS, HIDDEN, MOE_INTER), dtype=jnp.float32) * s
        shared_w_gate_up = jax.random.normal(ks[4], (2 * SHARED_INTER, HIDDEN), dtype=jnp.float32) * s
        shared_w_down = jax.random.normal(ks[5], (HIDDEN, SHARED_INTER), dtype=jnp.float32) * s
        return {'hidden_states': hidden_states, 'gate_w': gate_w, 'w_gate_up': w_gate_up, 'w_down': w_down, 'shared_w_gate_up': shared_w_gate_up, 'shared_w_down': shared_w_down}
    _L0_ffn_all = _L0_ffn_setup()
    _L0_ffn_in = {k: v for k, v in _L0_ffn_all.items() if k in ('gate_w', 'w_gate_up', 'w_down', 'shared_w_gate_up', 'shared_w_down')}
    del _L0_ffn_all
    return {'x': x, 'ctx_4096': ctx_4096, 'L0_ffn_gate_w': _L0_ffn_in['gate_w'], 'L0_ffn_w_gate_up': _L0_ffn_in['w_gate_up'], 'L0_ffn_w_down': _L0_ffn_in['w_down'], 'L0_ffn_shared_w_gate_up': _L0_ffn_in['shared_w_gate_up'], 'L0_ffn_shared_w_down': _L0_ffn_in['shared_w_down']}

def reference(x, ctx_4096, L0_ffn_gate_w, L0_ffn_w_gate_up, L0_ffn_w_down, L0_ffn_shared_w_gate_up, L0_ffn_shared_w_down):
    import jax
    import jax.numpy as jnp

    def _L0_xattn_ref(Q, K, V):
        import jax, jax.numpy as jnp
        import numpy as np
        H = 8
        C = 2

        def _autocorrelation(Q, K, V):
            B, L, D = Q.shape
            d = D // H
            q = Q.reshape(B, L, H, d).transpose(0, 2, 1, 3)
            k = K.reshape(B, L, H, d).transpose(0, 2, 1, 3)
            v = V.reshape(B, L, H, d).transpose(0, 2, 1, 3)
            qf = jnp.fft.fft(q, axis=2)
            kf = jnp.fft.fft(k, axis=2)
            corr = jnp.fft.ifft(qf * jnp.conj(kf), axis=2).real
            topk = int(C * np.log(L))
            w, idx = jax.lax.top_k(corr.transpose(0, 1, 3, 2), topk)
            w = jax.nn.softmax(w, axis=-1)
            pos = jnp.arange(L)[:, None]
            out = jnp.zeros_like(v)
            for i in range(topk):
                g = jnp.minimum(idx[:, :, None, :, i] + pos, L - 1)
                out = out + w[:, :, None, :, i] * jnp.take_along_axis(v, g, axis=2)
            return out.transpose(0, 2, 1, 3).reshape(B, L, D)
        return _autocorrelation(Q, K, V)

    def _L0_ffn_ref(hidden_states, gate_w, w_gate_up, w_down, shared_w_gate_up, shared_w_down):
        import jax, jax.numpy as jnp
        import numpy as np
        HIDDEN = 512
        MOE_INTER = 128
        SHARED_INTER = 512
        NUM_EXPERTS = 16
        TOP_K = 2

        def _moe_forward(x, gate_w, w_gate_up, w_down, shared_w_gate_up, shared_w_down):
            orig_shape = x.shape
            x2 = x.reshape(-1, orig_shape[-1])
            gu_s = x2 @ shared_w_gate_up.T
            g_s, u_s = jnp.split(gu_s, 2, axis=-1)
            shared_out = jax.nn.silu(g_s) * u_s @ shared_w_down.T
            logits = x2 @ gate_w.T
            probs = jax.nn.softmax(logits, axis=-1)
            topk_vals, topk_idx = jax.lax.top_k(probs, TOP_K)
            topk_vals = topk_vals / jnp.sum(topk_vals, axis=-1, keepdims=True)
            combine = jnp.sum(jax.nn.one_hot(topk_idx, NUM_EXPERTS, dtype=x2.dtype) * topk_vals[..., None], axis=1)
            gu = jnp.einsum('th,eih->eti', x2, w_gate_up)
            g, u = jnp.split(gu, 2, axis=-1)
            act = jax.nn.silu(g) * u
            out_e = jnp.einsum('eti,ehi->eth', act, w_down)
            moe_out = jnp.einsum('eth,te->th', out_e, combine)
            return (moe_out + shared_out).reshape(orig_shape)
        return _moe_forward(hidden_states, gate_w, w_gate_up, w_down, shared_w_gate_up, shared_w_down)
    x = x + _L0_xattn_ref(_layernorm(x, axis=-1), ctx_4096, ctx_4096)
    x = x + _L0_ffn_ref(_layernorm(x, axis=-1), L0_ffn_gate_w, L0_ffn_w_gate_up, L0_ffn_w_down, L0_ffn_shared_w_gate_up, L0_ffn_shared_w_down)
    return x

_drawn_inputs = setup_inputs


def setup_inputs(seed=0):
    import zlib

    import numpy as np

    out = dict(_drawn_inputs(seed))
    spreads = {}
    factors = {'L0_ffn_gate_w': 4.719,
     'L0_ffn_w_gate_up': 4.378,
     'L0_ffn_w_down': 4.408,
     'L0_ffn_shared_w_gate_up': 2.816,
     'L0_ffn_shared_w_down': 2.808}
    for name, (base, spread) in spreads.items():
        noise = np.random.default_rng([zlib.crc32(name.encode()), seed]).standard_normal(out[name].shape)
        drawn = base * np.exp(spread * noise) if base else spread * noise
        out[name] = jnp.asarray(drawn.astype(out[name].dtype))
    for name, factor in factors.items():
        out[name] = (out[name] * factor).astype(out[name].dtype)
    return out
```

```python
from contextlib import ExitStack

import numpy as np

import concourse.bass as bass
from concourse import mybir

F32 = mybir.dt.float32
I32 = mybir.dt.int32
U32 = mybir.dt.uint32
ALU = mybir.AluOpType
ACT = mybir.ActivationFunctionType
AX = mybir.AxisListType

P = 128
SEQS, L, D = 32, 64, 512
TOKENS = SEQS * L
PAIRS = TOKENS // P
KB = D // P
TOPK = 8
SEGS = 2 * KB
E = 16
INTER = 128
SHARED = 512
SB = SHARED // P
CHOICES = 2
SLOT_TILES = (CHOICES * TOKENS + E * (P - 1)) // P
JW = SLOT_TILES + 1
GROUPS = 4
GT = PAIRS // GROUPS
EPS = 1e-5
TAKEN = -3.0e38
YBUFS = 4


def spectrum_rows(seq, real):
    return seq * 32 + np.arange(32) + (0 if real else 64)


def forward(odd, context):
    t, r = np.arange(L)[:, None], np.arange(32)[None, :]
    angle = np.pi * (2 * r + odd) * t / L
    re, im = np.cos(angle), -np.sin(angle)
    if not odd:
        im[:, 0] = (-1.0) ** t[:, 0]
    if context and odd:
        re[-1] -= re.sum(0)
        im[-1] -= im.sum(0)
    if context and not odd:
        re[-1, 0] += L
    out = np.zeros((P, P))
    for s in range(2):
        out[s * L:(s + 1) * L, spectrum_rows(s, True)] = re
        out[s * L:(s + 1) * L, spectrum_rows(s, False)] = im
    return out


def inverse(odd, swapped, sign, scale):
    t, r = np.arange(L)[None, :], np.arange(32)[:, None]
    angle = np.pi * (2 * r + odd) * t / L
    if swapped:
        re = sign * 2 * np.sin(angle) / L
        im = -re
        if not odd:
            re[0], im[0] = 0.0, 0.0
    else:
        re = 2 * np.cos(angle) / L
        im = re.copy()
        if not odd:
            re[0], im[0] = 1 / L, (-1.0) ** t[0] / L
    out = np.zeros((P, P))
    for s in range(2):
        out[spectrum_rows(s, True), s * L:(s + 1) * L] = re * scale
        out[spectrum_rows(s, False), s * L:(s + 1) * L] = im * scale
    return out


CONSTANTS = [
    ("even", P), ("even_context", P), ("odd", P), ("odd_context", P),
    ("corr_plain", P), ("corr_swapped", P),
    ("out_even_plain", P), ("out_even_swapped", P), ("out_odd_plain", P), ("out_odd_swapped", P),
    ("identity", P), ("earlier", P), ("ones", P), ("count", P), ("tile_edge", E),
    ("token", PAIRS), ("minus_half", 1), ("eps", 1),
]


def constants():
    p = np.arange(P)
    values = {
        "even": forward(0, False), "even_context": forward(0, True),
        "odd": forward(1, False), "odd_context": forward(1, True),
        "corr_plain": inverse(0, False, 1, 1.0), "corr_swapped": inverse(0, True, 1, 1.0),
        "out_even_plain": inverse(0, False, 1, 0.5), "out_even_swapped": inverse(0, True, -1, 0.5),
        "out_odd_plain": inverse(1, False, 1, 0.5), "out_odd_swapped": inverse(1, True, -1, 0.5),
        "identity": np.eye(P), "earlier": np.triu(np.ones((P, P)), 1), "ones": np.ones((P, P)),
        "count": np.tile(p, (P, 1)), "tile_edge": np.tile(P * np.arange(E), (P, 1)),
        "token": p[:, None] + P * np.arange(PAIRS)[None, :], "minus_half": np.full((P, 1), -0.5), "eps": np.full((P, 1), EPS),
    }
    return np.concatenate([values[n].astype(np.float32) for n, _ in CONSTANTS], axis=1)


def build(nc, x, ctx, consts, gate, w_gu, w_down, sh_gu, sh_down, out):
    with ExitStack() as stack:
        def sb(name, shape, dt=F32):
            return stack.enter_context(nc.sbuf_tensor(name, shape, dt))

        sems = {}

        def sem(name):
            sems[name] = stack.enter_context(nc.semaphore(name))
            return sems[name]

        def wait(eng, s, value):
            if not (isinstance(value, int) and value <= 0):
                eng.wait_ge(s, value)

        def apart(eng, passed):
            eng.sem_inc(passed, 1)

        x2_rows = nc.dram_tensor("x2_rows", [TOKENS, D], F32, kind="Internal").ap()
        y_rows = nc.dram_tensor("y_rows", [SLOT_TILES * P, D], F32, kind="Internal").ap()

        const_sb = sb("const_sb", [P, consts.shape[1]])
        at, C = 0, {}
        for name, width in CONSTANTS:
            C[name] = const_sb[:, at:at + width]
            at += width
        resid = sb("resid", [P, PAIRS * D])
        x2T = sb("x2T", [P, PAIRS * KB * P])
        wgu_sb = sb("wgu_sb", [P, E * KB * 2 * INTER])
        shgu_sb = sb("shgu_sb", [P, KB * 2 * SHARED])
        gate_sb = sb("gate_sb", [P, KB * E])
        arena = sb("arena", [P, 21 * D])
        xg_sb = sb("xg_sb", [P, 2 * D])
        silu_sb = sb("silu_sb", [P, D])
        b_at = [0]

        def cut():
            b_at[0] += 1
            return arena[:, (b_at[0] - 1) * D:b_at[0] * D]

        ctx_in = [cut(), cut()]
        xn = silu_sb[:, :]
        ctx_even, ctx_even_sw = [cut(), cut()], [cut(), cut()]
        ctx_odd, ctx_odd_sw = [cut(), cut()], [cut(), cut()]
        prod_plain, prod_swapped = cut(), cut()
        expz, lagw, lagwT = cut(), cut(), cut()
        out_prod = [cut() for _ in range(4)]
        x2n = [cut(), cut()]
        x2T_tile = [xg_sb[:, 0:D], xg_sb[:, D:2 * D]]
        assert b_at[0] == 21
        wd_sb = arena[:, 0:E * D]
        shd_sb = arena[:, E * D:(E + SB) * D]
        totals = arena[:, (E + SB) * D:(E + SB) * D + E * PAIRS]
        cumul = arena[:, (E + SB) * D + E * PAIRS:(E + SB + 1) * D]
        LAST_GU = (E // 2 - 1) * 2 * KB * 2 * INTER
        sh_act = wgu_sb[:, LAST_GU:LAST_GU + SB * D]
        xgT = [x2T[:, 0:D], x2T[:, D:2 * D]]
        y_out = [x2T[:, 2 * D:3 * D], x2T[:, 3 * D:4 * D]]
        xg = [xg_sb[:, 0:D], xg_sb[:, D:2 * D]]
        act_sb = sb("act_sb", [P, P])
        actT_sb = sb("actT_sb", [P, P])
        y_in = [wgu_sb[:, i * D:(i + 1) * D] for i in range(YBUFS)]

        stats = [sb(f"stats{i}", [P, 6]) for i in range(2)]
        meanvar = [sb(f"meanvar{i}", [P, 2]) for i in range(2)]
        rstd = [sb(f"rstd{i}", [P, 1]) for i in range(2)]
        veps = [sb(f"veps{i}", [P, 1]) for i in range(2)]
        top_v = sb("top_v", [P, SEGS * TOPK])
        top_e = sb("top_e", [P, SEGS * TOPK])
        top_s = sb("top_s", [P, SEGS])
        top_r = sb("top_r", [P, SEGS])
        logits = sb("logits", [P, PAIRS * E])
        r_val = sb("r_val", [P, PAIRS * 8])
        r_idx = sb("r_idx", [P, PAIRS * 8], U32)
        r_idxf = sb("r_idxf", [P, CHOICES * PAIRS])
        r_exp = sb("r_exp", [P, PAIRS])
        r_sum = sb("r_sum", [P, PAIRS])
        r_w = sb("r_w", [P, CHOICES * PAIRS])
        chosen = [xg_sb[:, k * PAIRS * E:(k + 1) * PAIRS * E] for k in range(CHOICES)]
        chosen_any = xg_sb[:, 2 * PAIRS * E:3 * PAIRS * E]
        route_tmp = xg_sb[:, 3 * PAIRS * E:4 * PAIRS * E]
        e_before = sb("e_before", [P, E])
        e_count = sb("e_count", [P, E])
        e_tiles = sb("e_tiles", [P, E])
        e_cum = sb("e_cum", [P, E])
        e_start = sb("e_start", [P, E])
        pos_f = sb("pos_f", [P, CHOICES * PAIRS])
        pos_i = sb("pos_i", [P, CHOICES * PAIRS], I32)
        hilo_i = sb("hilo_i", [P, CHOICES * PAIRS], I32)
        hi_f = sb("hi_f", [P, CHOICES * PAIRS])
        lo_f = sb("lo_f", [P, CHOICES * PAIRS])
        tile_e = sb("tile_e", [P, JW])
        tile_ei = sb("tile_ei", [P, JW], I32)
        lane_hot = [xg_sb[:, k * P:(k + 1) * P] for k in range(CHOICES)]
        tile_hot = [xg_sb[:, CHOICES * P + k * 2 * JW:CHOICES * P + (k + 1) * 2 * JW] for k in range(CHOICES)]
        slot_token = sb("slot_token", [P, JW], I32)
        slot_w = sb("slot_w", [P, JW])
        gidx = [sb(f"gidx{i}", [P, 1], I32) for i in range(YBUFS)]

        bank = [stack.enter_context(nc.psum_tensor(f"bank{i}", [P, D], F32)) for i in range(8)]
        ps_x, ps_even, ps_odd, ps_corr, ps_T, ps_w_even, ps_w_odd, ps_out = bank

        const_loaded = sem("const_loaded")
        x_loaded, ctx_loaded = [sem("x_loaded0"), sem("x_loaded1")], [sem("ctx_loaded0"), sem("ctx_loaded1")]
        gate_loaded, wgu_loaded, shgu_loaded = sem("gate_loaded"), sem("wgu_loaded"), sem("shgu_loaded")
        wd_loaded, shd_loaded = sem("wd_loaded"), sem("shd_loaded")
        x2_stored = [sem("x2_stored0"), sem("x2_stored1")]
        stats_done = [sem("x_stats_done"), sem("resid_stats_done")]
        meanvar_ready = [sem("x_meanvar_ready"), sem("resid_meanvar_ready")]
        veps_ready = [sem("x_veps_ready"), sem("resid_veps_ready")]
        rstd_ready = [sem("x_rstd_ready"), sem("resid_rstd_ready")]
        xn_ready, x_spectrum = sem("xn_ready"), sem("x_spectrum")
        ctx_even_psum, ctx_even_ready = sem("ctx_even_psum"), sem("ctx_even_ready")
        ctx_odd_psum, ctx_odd_ready = sem("ctx_odd_psum"), sem("ctx_odd_ready")
        products_ready, corr_psum = sem("products_ready"), sem("corr_psum")
        maxima_ready, centered, lags_marked = sem("maxima_ready"), sem("centered"), sem("lags_marked")
        exp_ready, top_sum_ready, masked = sem("exp_ready"), sem("top_sum_ready"), sem("masked")
        top_r_ready = sem("top_r_ready")
        lagw_ready, lagwT_psum, lagwT_ready = sem("lagw_ready"), sem("lagwT_psum"), sem("lagwT_ready")
        w_even_psum, w_odd_psum = sem("w_even_psum"), sem("w_odd_psum")
        out_products_ready, out_psum, resid_ready = sem("out_products_ready"), sem("out_psum"), sem("resid_ready")
        x2n_ready, x2T_psum, x2T_ready, x2T_kept = sem("x2n_ready"), sem("x2T_psum"), sem("x2T_ready"), sem("x2T_kept")
        logits_psum, logits_ready = sem("logits_psum"), sem("logits_ready")
        route_step, route_diff, route_exp = sem("route_step"), sem("route_diff"), sem("route_exp")
        chosen_ready, counts_psum = sem("chosen_ready"), sem("counts_psum")
        hot_ready, slots_psum, slots_ready = sem("hot_ready"), sem("slots_psum"), sem("slots_ready")
        tile_e_ready, pos_ready = sem("tile_e_ready"), sem("pos_ready")
        sh_gate_psum, sh_up_psum, sh_silu = sem("sh_gate_psum"), sem("sh_up_psum"), sem("sh_silu")
        sh_act_ready, sh_out_psum, sh_added = sem("sh_act_ready"), sem("sh_out_psum"), sem("sh_added")
        gidx_ready = sem("gidx_ready")
        gathered = [sem("gathered0"), sem("gathered1")]
        xgT_psum, xgT_ready, gu_psum, silu_ready = sem("xgT_psum"), sem("xgT_ready"), sem("gu_psum"), sem("silu_ready")
        act_ready, actT_psum, actT_ready = sem("act_ready"), sem("actT_psum"), sem("actT_ready")
        down_psum, y_ready = sem("down_psum"), sem("y_ready")
        y_stored = [sem("y_stored0"), sem("y_stored1")]
        y_gathered = [sem(f"y_gathered{i}") for i in range(YBUFS)]
        yidx_ready, y_half_added, y_added = sem("yidx_ready"), sem("y_half_added"), sem("y_added")
        out_stored = sem("out_stored")
        dve_passed, pool_passed = sem("dve_passed"), sem("pool_passed")

        def tile_of(tensor, p):
            return tensor[:, bass.ds(p * D, D)]

        def segs(ap):
            return ap.rearrange("p (s l) -> p s l", s=SEGS)

        def schedule(iteration):
            for i in range(0, 4):
                iteration(i // 2, i % 2, i)
            return range(2, (PAIRS - 2) // 2), [(i // 2, i % 2, i) for i in range(PAIRS - 2, PAIRS + 2)]

        def live(n, d):
            return n is None or 0 <= n + d < PAIRS

        def pair(h, b, d):
            return 2 * h + (b + d), (b + d) % 2

        def half(h, b, d):
            return h + (b + d) // 2

        def run(eng, iteration):
            hs, last = schedule(iteration)
            with eng.Fori(hs.start, hs.stop) as h:
                for b in range(2):
                    iteration(h, b, None)
            for h, b, n in last:
                iteration(h, b, n)

        block = stack.enter_context(nc.Block())

        @block.sync
        def _(sp):
            def load_pair(h, b):
                p = 2 * h + b
                wait(sp, ctx_odd_psum, p - 1)
                sp.dma_start(tile_of(resid, p), x[bass.ds(p * P, P), :]).then_inc(x_loaded[b], 16)
                sp.dma_start(ctx_in[b], ctx[bass.ds(p * P, P), :]).then_inc(ctx_loaded[b], 16)

            def load_expert_pair(h):
                width = 2 * KB * 2 * INTER
                sp.dma_start(wgu_sb[:, bass.ds(h * width, width)],
                             w_gu[:, bass.ds(h * width, width)]).then_inc(wgu_loaded, 16)

            def iteration(h, b, n):
                if n is None or n + 2 < PAIRS:
                    load_pair(h + 1, b)
                if live(n, -2):
                    p, pb = pair(h, b, -2)
                    sp.wait_ge(x2n_ready, p + 1)
                    sp.dma_start(x2_rows[bass.ds(p * P, P), :], x2n[pb]).then_inc(x2_stored[pb], 16)
                if b == 1 and (n is None or n == 3):
                    sp.wait_ge(wgu_loaded, 16 * h)
                    load_expert_pair(h)

            sp.dma_start(tile_of(resid, 0), x[0:P, :]).then_inc(x_loaded[0], 16)
            sp.dma_start(const_sb[:, :], consts[:, :]).then_inc(const_loaded, 16)
            sp.dma_start(ctx_in[0], ctx[0:P, :]).then_inc(ctx_loaded[0], 16)
            load_pair(0, 1)
            sp.dma_start(gate_sb[:, :], gate[:, :]).then_inc(gate_loaded, 16)
            load_expert_pair(0)
            run(sp, iteration)
            sp.dma_start(shgu_sb[:, :], sh_gu[:, :]).then_inc(shgu_loaded, 16)
            sp.wait_ge(logits_psum, PAIRS)
            sp.wait_ge(x2T_kept, PAIRS)
            for b in range(2):
                sp.wait_ge(x2_stored[b], 16 * PAIRS // 2)
            sp.dma_start(shd_sb, sh_down[:, :]).then_inc(shd_loaded, 16)
            sp.dma_start(wd_sb, w_down[:, :]).then_inc(wd_loaded, 16)
            sp.wait_ge(sh_out_psum, GT)
            sp.wait_ge(wgu_loaded, 16 * (E // 2 - 1))
            load_expert_pair(E // 2 - 1)

            def store_y(h, b):
                j = 2 * h + b
                sp.wait_ge(y_ready, j + 1)
                sp.dma_start(y_rows[bass.ds(j * P, P), :], y_out[b]).then_inc(y_stored[b], 16)

            with sp.Fori(0, SLOT_TILES // 2) as h:
                for b in range(2):
                    store_y(h, b)
            store_y(SLOT_TILES // 2, 0)
            for t in range(GT):
                sp.wait_ge(y_added, t + 1)
                sp.dma_start(out[t * P:(t + 1) * P, :], tile_of(resid, t)).then_inc(out_stored, 16)
            with sp.Fori(GT, PAIRS) as t:
                sp.wait_ge(sh_added, t + 1)
                sp.dma_start(out[bass.ds(t * P, P), :], tile_of(resid, t)).then_inc(out_stored, 16)
            sp.wait_ge(out_stored, 16 * PAIRS)

        @block.tensor
        def _(pe):
            mm = nc.tensor.matmul

            def iteration(h, b, n):
                if live(n, 0):
                    p, _ = pair(h, b, 0)
                    pe.wait_ge(xn_ready, p + 1)
                    wait(pe, products_ready, p)
                    mm(ps_x[:, :], C["even"], xn, start=True, stop=True).then_inc(x_spectrum, 1)
                    pe.wait_ge(ctx_loaded[b], 16 * (h + 1))
                    wait(pe, ctx_even_ready, p)
                    mm(ps_even[:, :], C["even_context"], ctx_in[b], start=True, stop=True).then_inc(ctx_even_psum, 1)
                    wait(pe, ctx_odd_ready, p)
                    mm(ps_odd[:, :], C["odd_context"], ctx_in[b], start=True, stop=True).then_inc(ctx_odd_psum, 1)
                if live(n, -1):
                    p, _ = pair(h, b, -1)
                    pe.wait_ge(lagw_ready, p + 1)
                    wait(pe, x2T_ready, p - 1)
                    for c in range(KB):
                        cols = slice(c * P, (c + 1) * P)
                        last = nc.tensor.transpose(ps_T[:, cols], lagw[:, cols], C["identity"])
                    last.then_inc(lagwT_psum, 1)
                if live(n, 0):
                    p, _ = pair(h, b, 0)
                    pe.wait_ge(products_ready, p + 1)
                    wait(pe, lags_marked, p)
                    for c in range(KB):
                        cols = slice(c * P, (c + 1) * P)
                        mm(ps_corr[:, cols], prod_plain[:, cols], C["corr_plain"], start=True, stop=False)
                        last = mm(ps_corr[:, cols], prod_swapped[:, cols], C["corr_swapped"], start=False, stop=True)
                    last.then_inc(corr_psum, 1)
                if live(n, -1):
                    p, _ = pair(h, b, -1)
                    pe.wait_ge(lagwT_ready, p + 1)
                    wait(pe, out_products_ready, p)
                    mm(ps_w_even[:, :], C["even"], lagwT, start=True, stop=True).then_inc(w_even_psum, 1)
                    wait(pe, logits_ready, p - 1)
                    mm(ps_w_odd[:, :], C["odd"], lagwT, start=True, stop=True).then_inc(w_odd_psum, 1)
                if live(n, -2):
                    p, pb = pair(h, b, -2)
                    pe.wait_ge(x2n_ready, p + 1)
                    wait(pe, lagwT_ready, p + 2 if n is None else min(n, PAIRS))
                    for c in range(KB):
                        cols = slice(c * P, (c + 1) * P)
                        last = nc.tensor.transpose(ps_T[:, cols], x2n[pb][:, cols], C["identity"])
                    last.then_inc(x2T_psum, 1)
                if live(n, -1):
                    p, _ = pair(h, b, -1)
                    pe.wait_ge(out_products_ready, p + 1)
                    wait(pe, resid_ready, p)
                    parts = ("out_even_plain", "out_even_swapped", "out_odd_plain", "out_odd_swapped")
                    for m, name in enumerate(parts):
                        last = mm(ps_out[:, :], C[name], out_prod[m], start=m == 0, stop=m == len(parts) - 1)
                    last.then_inc(out_psum, 1)
                if live(n, -2):
                    p, pb = pair(h, b, -2)
                    pe.wait_ge(x2T_ready, p + 1)
                    for c in range(KB):
                        last = mm(ps_w_odd[:, 0:E], x2T_tile[pb][:, c * P:(c + 1) * P], gate_sb[:, c * E:(c + 1) * E],
                                  start=c == 0, stop=c == KB - 1)
                    last.then_inc(logits_psum, 1)

            def shared_group(g, first=False):
                def tokens(c):
                    cols = x2T[:, bass.ds(g * GT * D, GT * D)]
                    return cols.rearrange("p (t c n) -> p c t n", t=GT, c=KB)[:, c]
                for m in range(SB):
                    n = g * SB + m
                    for part, (ps, s, freed) in enumerate(((bank[0], sh_gate_psum, sh_silu), (bank[1], sh_up_psum, sh_act_ready))):
                        wait(pe, freed, n)
                        for c in range(KB):
                            col = c * 2 * SHARED + part * SHARED + m * P
                            last = mm(ps[:, :].rearrange("p (t n) -> p t n", t=GT), shgu_sb[:, col:col + P], tokens(c),
                                      start=c == 0, stop=c == KB - 1)
                        last.then_inc(s, 1)
                if first:
                    pe.wait_ge(shd_loaded, 16)
                pe.wait_ge(sh_act_ready, (g + 1) * SB)
                for t in range(GT):
                    n = g * GT + t
                    wait(pe, sh_added, n - 1)
                    for m in range(SB):
                        last = mm(bank[2 + t % 2][:, :], sh_act[:, m * D + t * P:m * D + (t + 1) * P],
                                  shd_sb[:, m * D:(m + 1) * D], start=m == 0, stop=m == SB - 1)
                    last.then_inc(sh_out_psum, 1)

            pe.wait_ge(const_loaded, 16)
            pe.wait_ge(gate_loaded, 16)
            run(pe, iteration)

            pe.wait_ge(logits_ready, PAIRS)
            pe.wait_ge(resid_ready, PAIRS)
            pe.wait_ge(x2T_kept, PAIRS)
            pe.wait_ge(shgu_loaded, 16)
            def counts():
                pe.wait_ge(chosen_ready, 1)
                mm(bank[4][:, 0:PAIRS * E], C["earlier"], chosen_any, start=True, stop=True)
                mm(bank[5][:, 0:PAIRS * E], C["ones"], chosen_any, start=True, stop=True).then_inc(counts_psum, 1)

            def invert(t, first=False):
                for k in range(CHOICES):
                    pe.wait_ge(hot_ready, t * CHOICES + k + 1)
                    mm(bank[6][:, 0:2 * JW], lane_hot[k], tile_hot[k],
                       start=first and k == 0, stop=True, skip_group_check=True).then_inc(slots_psum, 1)

            shared_group(0, first=True)
            counts()
            invert(0, first=True)
            with pe.Fori(1, PAIRS) as t:
                invert(t)

            def expert(h, b, n):
                j = 2 * h + b
                if n is None or n > 0:
                    pe.wait_ge(act_ready, j)
                    wait(pe, actT_ready, j - 1)
                    nc.tensor.transpose(bank[5][:, 0:P], act_sb[:, :], C["identity"]).then_inc(actT_psum, 1)
                if n is None or n < SLOT_TILES:
                    e = pe.value_load(tile_ei[0:1, bass.ds(j, 1)], min_val=0, max_val=E - 1)
                    pe.wait_ge(xgT_ready, j + 1)
                    wait(pe, act_ready, j - 1)
                    for c in range(KB):
                        last = mm(bank[1 + b][:, 0:2 * INTER], xgT[b][:, c * P:(c + 1) * P],
                                  wgu_sb[:, bass.ds(e * (KB * 2 * INTER) + c * 2 * INTER, 2 * INTER)],
                                  start=c == 0, stop=c == KB - 1)
                    last.then_inc(gu_psum, 1)
                if n is None or n > 0:
                    e = pe.value_load(tile_ei[0:1, bass.ds(j - 1, 1)], min_val=0, max_val=E - 1)
                    pe.wait_ge(actT_ready, j)
                    wait(pe, y_ready, j - 2)
                    mm(bank[3 + (1 - b)][:, :], actT_sb[:, :], wd_sb[:, bass.ds(e * D, D)],
                       start=True, stop=True).then_inc(down_psum, 1)
                if n is None or n + 1 < SLOT_TILES:
                    q = (b + 1) % 2
                    pe.wait_ge(gathered[q], 16 * (h + 1 + (b + 1) // 2))
                    for c in range(KB):
                        cols = slice(c * P, (c + 1) * P)
                        last = nc.tensor.transpose(bank[0][:, cols], xg[q][:, cols], C["identity"])
                    last.then_inc(xgT_psum, 1)

            pe.wait_ge(tile_e_ready, 1)
            pe.wait_ge(wd_loaded, 16)
            pe.wait_ge(wgu_loaded, 16 * E // 2)
            pe.wait_ge(slots_ready, 1)
            pe.wait_ge(gathered[0], 16)
            for c in range(KB):
                cols = slice(c * P, (c + 1) * P)
                last = nc.tensor.transpose(bank[0][:, cols], xg[0][:, cols], C["identity"])
            last.then_inc(xgT_psum, 1)
            for n in range(2):
                expert(0, n, n)
            with pe.Fori(1, SLOT_TILES // 2) as h:
                for b in range(2):
                    expert(h, b, None)
            for n in range(SLOT_TILES - 1, SLOT_TILES + 1):
                expert(n // 2, n % 2, n)

            pe.wait_ge(y_ready, SLOT_TILES)
            with pe.Fori(1, GROUPS) as g:
                shared_group(g)

        @block.scalar
        def _(act):
            copy = nc.scalar.copy

            def iteration(h, b, n):
                if live(n, 0):
                    p, _ = pair(h, b, 0)
                    act.wait_ge(ctx_even_psum, p + 1)
                    wait(act, out_products_ready, p - 1)
                    copy(ctx_even[b], ps_even[:, :])
                    copy(ctx_even_sw[b][0:64, :], ps_even[64:128, :])
                    copy(ctx_even_sw[b][64:128, :], ps_even[0:64, :]).then_inc(ctx_even_ready, 1)
                if live(n, -1):
                    p, _ = pair(h, b, -1)
                    act.wait_ge(lagwT_psum, p + 1)
                    wait(act, w_odd_psum, p)
                    copy(lagwT, ps_T[:, :]).then_inc(lagwT_ready, 1)
                if live(n, 0):
                    p, _ = pair(h, b, 0)
                    act.wait_ge(ctx_odd_psum, p + 1)
                    copy(ctx_odd[b], ps_odd[:, :])
                    copy(ctx_odd_sw[b][0:64, :], ps_odd[64:128, :])
                    copy(ctx_odd_sw[b][64:128, :], ps_odd[0:64, :]).then_inc(ctx_odd_ready, 1)
                if live(n, -2):
                    p, pb = pair(h, b, -2)
                    act.wait_ge(x2T_psum, p + 1)
                    wait(act, x2T_kept, p - 1)
                    wait(act, logits_psum, p - 1)
                    copy(x2T_tile[pb], ps_T[:, :]).then_inc(x2T_ready, 1)
                if live(n, 0):
                    p, _ = pair(h, b, 0)
                    act.wait_ge(centered, p + 1)
                    nc.scalar.activation(top_e[:, :], top_e[:, :], ACT.Exp)
                    nc.scalar.activation(expz, expz, ACT.Exp).then_inc(exp_ready, 1)
                if live(n, -2):
                    p, _ = pair(h, b, -2)
                    act.wait_ge(logits_psum, p + 1)
                    copy(logits[:, bass.ds(p * E, E)], ps_w_odd[:, 0:E]).then_inc(logits_ready, 1)

            run(act, iteration)

            act.wait_ge(route_diff, 1)
            nc.scalar.activation(r_exp[:, :], r_exp[:, :], ACT.Exp).then_inc(route_exp, 1)

            def shared_silu(g):
                for m in range(SB):
                    n = g * SB + m
                    act.wait_ge(sh_gate_psum, n + 1)
                    wait(act, sh_act_ready, n)
                    nc.scalar.activation(silu_sb[:, :], bank[0][:, :], ACT.Silu).then_inc(sh_silu, 1)

            shared_silu(0)

            def gathered_T(h, b):
                j = 2 * h + b
                act.wait_ge(xgT_psum, j + 1)
                wait(act, gu_psum, j - 1)
                copy(xgT[b], bank[0][:, :]).then_inc(xgT_ready, 1)

            def expert(h, b, n):
                j = 2 * h + b
                act.wait_ge(gu_psum, j + 1)
                wait(act, act_ready, j)
                nc.scalar.activation(silu_sb[:, 0:INTER], bank[1 + b][:, 0:INTER], ACT.Silu).then_inc(silu_ready, 1)
                if n is None or n + 1 < SLOT_TILES:
                    gathered_T(h + (b + 1) // 2, (b + 1) % 2)

            act.wait_ge(sh_out_psum, GT)
            gathered_T(0, 0)
            for n in range(2):
                expert(0, n, n)
            with act.Fori(1, SLOT_TILES // 2) as h:
                for b in range(2):
                    expert(h, b, None)
            expert(SLOT_TILES // 2, 0, SLOT_TILES - 1)

            with act.Fori(1, GROUPS) as g:
                shared_silu(g)

        @block.vector
        def _(dve):
            tt, ts, stt = nc.vector.tensor_tensor, nc.vector.tensor_scalar, nc.vector.scalar_tensor_tensor

            def moments(which, src, p):
                nc.vector.bn_stats(stats[which][:, :], src).then_inc(stats_done[which], 1)
                dve.wait_ge(stats_done[which], p + 1)
                apart(dve, dve_passed)
                nc.vector.bn_aggr(meanvar[which][:, :], stats[which][:, :]).then_inc(meanvar_ready[which], 1)

            def normalise(which, dst, src, p, done):
                dve.wait_ge(rstd_ready[which], p + 1)
                ts(dst, src, meanvar[which][:, 0:1], rstd[which][:, :], ALU.subtract, ALU.mult).then_inc(done, 1)

            def iteration(h, b, n):
                if live(n, 1):
                    p, pb = pair(h, b, 1)
                    dve.wait_ge(x_loaded[pb], 16 * (half(h, b, 1) + 1))
                    apart(dve, dve_passed)
                    moments(0, tile_of(resid, p), p)
                if live(n, 0):
                    p, _ = pair(h, b, 0)
                    dve.wait_ge(x_spectrum, p + 1)
                    dve.wait_ge(ctx_even_ready, p + 1)
                    tt(prod_plain, ps_x[:, :], ctx_even[b], ALU.mult)
                    tt(prod_swapped, ps_x[:, :], ctx_even_sw[b], ALU.mult).then_inc(products_ready, 1)
                if live(n, 1):
                    p, _ = pair(h, b, 1)
                    normalise(0, xn, tile_of(resid, p), p, xn_ready)
                if live(n, -1):
                    p, pb = pair(h, b, -1)
                    dve.wait_ge(w_even_psum, p + 1)
                    tt(out_prod[0], ps_w_even[:, :], ctx_even[pb], ALU.mult)
                    tt(out_prod[1], ps_w_even[:, :], ctx_even_sw[pb], ALU.mult)
                    dve.wait_ge(w_odd_psum, p + 1)
                    dve.wait_ge(ctx_odd_ready, p + 1)
                    tt(out_prod[2], ps_w_odd[:, :], ctx_odd[pb], ALU.mult)
                    tt(out_prod[3], ps_w_odd[:, :], ctx_odd_sw[pb], ALU.mult).then_inc(out_products_ready, 1)
                if live(n, 0):
                    p, _ = pair(h, b, 0)
                    dve.wait_ge(corr_psum, p + 1)
                    apart(dve, dve_passed)
                    lags, tops = segs(ps_corr[:, :]), segs(top_v[:, :])
                    for s in range(SEGS):
                        last = nc.vector.max(tops[:, s], lags[:, s])
                    last.then_inc(maxima_ready, 1)
                    dve.wait_ge(maxima_ready, p + 1)
                    largest = tops[:, :, 0:1]
                    tt(segs(top_e[:, :]), tops, largest.to_broadcast([P, SEGS, TOPK]), ALU.subtract)
                    tt(segs(expz), lags, largest.to_broadcast([P, SEGS, L]), ALU.subtract).then_inc(centered, 1)
                    for s in range(SEGS):
                        last = nc.vector.match_replace(segs(lagw)[:, s], tops[:, s], lags[:, s], TAKEN)
                    last.then_inc(lags_marked, 1)
                    dve.wait_ge(exp_ready, p + 1)
                    nc.vector.reduce_sum(top_s[:, :], segs(top_e[:, :]), axis=AX.X).then_inc(top_sum_ready, 1)
                    dve.wait_ge(lags_marked, p + 1)
                    stt(lagw, lagw, TAKEN, expz, ALU.is_equal, ALU.mult).then_inc(masked, 1)
                    dve.wait_ge(top_sum_ready, p + 1)
                    nc.vector.reciprocal(top_r[:, :], top_s[:, :]).then_inc(top_r_ready, 1)
                if live(n, -1):
                    p, pb = pair(h, b, -1)
                    dve.wait_ge(out_psum, p + 1)
                    tt(tile_of(resid, p), ps_out[:, :], tile_of(resid, p), ALU.add).then_inc(resid_ready, 1)
                    dve.wait_ge(resid_ready, p + 1)
                    apart(dve, dve_passed)
                    moments(1, tile_of(resid, p), p)
                    wait(dve, x2T_psum, p - 1)
                    wait(dve, x2_stored[pb], 16 * half(h, b, -1))
                    normalise(1, x2n[pb], tile_of(resid, p), p, x2n_ready)

            dve.wait_ge(const_loaded, 16)
            dve.wait_ge(x_loaded[0], 16)
            moments(0, tile_of(resid, 0), 0)
            normalise(0, xn, tile_of(resid, 0), 0, xn_ready)
            run(dve, iteration)

            steps = [0]

            def then(ins):
                steps[0] += 1
                ins.then_inc(route_step, 1)
                dve.wait_ge(route_step, steps[0])

            def by_expert(ap):
                return ap.rearrange("p (t e) -> p t e", e=E)

            def expert_major(ap):
                return ap.rearrange("p (e t) -> p e t", e=E)

            def over(ap, dims, axis):
                return ap.unsqueeze(axis).to_broadcast(dims)

            dve.wait_ge(logits_ready, PAIRS)
            dve.wait_ge(x2T_kept, PAIRS)
            vals, idx = r_val[:, :].rearrange("p (t v) -> p t v", v=8), r_idx[:, :].rearrange("p (t v) -> p t v", v=8)
            log_t = by_expert(logits[:, :])
            for t in range(PAIRS):
                last = nc.vector.max(vals[:, t], log_t[:, t])
            then(last)
            for t in range(PAIRS):
                last = nc.vector.max_index(idx[:, t], vals[:, t], log_t[:, t])
            tt(r_exp[:, :], vals[:, :, 1], vals[:, :, 0], ALU.subtract).then_inc(route_diff, 1)
            then(last)
            idxf = r_idxf[:, :].rearrange("p (k t) -> p k t", k=CHOICES)
            then(nc.vector.tensor_copy(idxf, idx[:, :, 0:CHOICES].rearrange("p t k -> p k t")))
            dims = [P, PAIRS, E]
            for k in range(CHOICES):
                last = tt(by_expert(chosen[k]), over(C["count"][:, 0:E], dims, 1), over(idxf[:, k], dims, 2), ALU.is_equal)
            then(last)
            tt(chosen_any, chosen[0], chosen[1], ALU.add).then_inc(chosen_ready, 1)
            wts = r_w[:, :].rearrange("p (k t) -> p k t", k=CHOICES)
            dve.wait_ge(route_exp, 1)
            then(ts(r_sum[:, :], r_exp[:, :], 1.0, None, ALU.add))
            then(nc.vector.reciprocal(wts[:, 0], r_sum[:, :]))
            then(tt(wts[:, 1], r_exp[:, :], wts[:, 0], ALU.mult))

            def shared_multiply(g):
                for m in range(SB):
                    n = g * SB + m
                    dve.wait_ge(sh_silu, n + 1)
                    dve.wait_ge(sh_up_psum, n + 1)
                    if m == 0:
                        wait(dve, sh_out_psum, g * GT)
                    tt(sh_act[:, m * D:(m + 1) * D], bank[1][:, :], silu_sb[:, :], ALU.mult).then_inc(sh_act_ready, 1)

            def shared_add(g):
                for t in range(GT):
                    n = g * GT + t
                    dve.wait_ge(sh_out_psum, n + 1)
                    dst = tile_of(resid, n)
                    tt(dst, bank[2 + t % 2][:, :], dst, ALU.add).then_inc(sh_added, 1)

            dve.wait_ge(shd_loaded, 16)
            shared_multiply(0)
            shared_add(0)

            dve.wait_ge(counts_psum, 1)
            totals3, cumul3 = expert_major(totals), expert_major(cumul)
            then(nc.vector.tensor_copy(totals3, by_expert(bank[5][:, 0:PAIRS * E]).rearrange("p t e -> p e t")))
            then(nc.vector.tensor_tensor_scan(cumul, C["ones"][:, 0:1].to_broadcast([P, E * PAIRS]), totals, 0.0, ALU.mult, ALU.add))
            nc.vector.memset(e_before[:, 0:1], 0.0)
            then(nc.vector.tensor_copy(e_before[:, 1:E], cumul3[:, 0:E - 1, PAIRS - 1]))
            then(tt(e_count[:, :], cumul3[:, :, PAIRS - 1], e_before[:, :], ALU.subtract))
            edges = expert_major(route_tmp)
            then(tt(edges, over(e_count[:, :], [P, E, E], 2), over(C["tile_edge"], [P, E, E], 1), ALU.is_gt))
            then(nc.vector.reduce_sum(e_tiles[:, :], edges, axis=AX.X))
            then(nc.vector.tensor_tensor_scan(e_cum[:, :], C["ones"][:, 0:E], e_tiles[:, :], 0.0, ALU.mult, ALU.add))
            then(tt(e_start[:, :], e_cum[:, :], e_tiles[:, :], ALU.subtract))
            then(stt(e_start[:, :], e_start[:, :], float(P), e_before[:, :], ALU.mult, ALU.subtract))
            then(tt(cumul, cumul, totals, ALU.subtract))
            then(tt(cumul3, cumul3, over(e_start[:, :], [P, E, PAIRS], 2), ALU.add))
            then(tt(by_expert(totals), by_expert(bank[4][:, 0:PAIRS * E]), cumul3.rearrange("p e t -> p t e"), ALU.add))
            pos = pos_f[:, :].rearrange("p (k t) -> p k t", k=CHOICES)
            for k in range(CHOICES):
                then(tt(route_tmp, chosen[k], totals, ALU.mult))
                then(nc.vector.reduce_sum(pos[:, k], by_expert(route_tmp), axis=AX.X))
            nc.vector.tensor_copy(pos_i[:, :], pos_f[:, :]).then_inc(pos_ready, 1)
            dve.wait_ge(pos_ready, 1)
            then(nc.vector.tensor_scalar(hilo_i[:, :], pos_i[:, :], 7, None, ALU.logical_shift_right))
            then(nc.vector.tensor_copy(hi_f[:, :], hilo_i[:, :]))
            then(nc.vector.tensor_scalar(hilo_i[:, :], pos_i[:, :], P - 1, None, ALU.bitwise_and))
            then(nc.vector.tensor_copy(lo_f[:, :], hilo_i[:, :]))
            step = PAIRS
            for j in range(0, JW, step):
                ended = route_tmp.rearrange("p (j e) -> p j e", e=E)
                then(tt(ended, over(e_cum[:, :], [P, step, E], 1), over(C["count"][:, j:j + step], [P, step, E], 2), ALU.is_le))
                then(nc.vector.reduce_sum(tile_e[:, j:j + step], ended, axis=AX.X))
            then(nc.vector.tensor_scalar(tile_e[:, :], tile_e[:, :], float(E - 1), None, ALU.min))
            nc.vector.tensor_copy(tile_ei[:, :], tile_e[:, :]).then_inc(tile_e_ready, 1)

            hi, lo = hi_f[:, :].rearrange("p (k t) -> p k t", k=CHOICES), lo_f[:, :].rearrange("p (k t) -> p k t", k=CHOICES)

            def one_hots(t):
                for k in range(CHOICES):
                    wait(dve, slots_psum, (t - 1) * CHOICES + k + 1)
                    ts(lane_hot[k], C["count"], lo[:, k, bass.ds(t, 1)], None, ALU.is_equal)
                    ts(tile_hot[k][:, 0:JW], C["count"][:, 0:JW], hi[:, k, bass.ds(t, 1)],
                       C["token"][:, bass.ds(t, 1)], ALU.is_equal, ALU.mult)
                    ts(tile_hot[k][:, JW:2 * JW], C["count"][:, 0:JW], hi[:, k, bass.ds(t, 1)],
                       wts[:, k, bass.ds(t, 1)], ALU.is_equal, ALU.mult).then_inc(hot_ready, 1)

            one_hots(0)
            with dve.Fori(1, PAIRS) as t:
                one_hots(t)
            dve.wait_ge(slots_psum, CHOICES * PAIRS)
            nc.vector.tensor_copy(slot_w[:, :], bank[6][:, JW:2 * JW])
            nc.vector.tensor_copy(slot_token[:, :], bank[6][:, 0:JW]).then_inc(slots_ready, 1)
            dve.wait_ge(slots_ready, 1)

            def expert(h, b, n):
                j = 2 * h + b
                if n is None or n > 0:
                    dve.wait_ge(actT_psum, j)
                    wait(dve, down_psum, j - 1)
                    nc.vector.tensor_copy(actT_sb[:, :], bank[5][:, 0:P]).then_inc(actT_ready, 1)
                if n is None or n < SLOT_TILES:
                    dve.wait_ge(silu_ready, j + 1)
                    stt(act_sb[:, :], bank[1 + b][:, INTER:2 * INTER], slot_w[:, bass.ds(j, 1)], silu_sb[:, 0:INTER],
                        ALU.mult, ALU.mult).then_inc(act_ready, 1)
                if n is None or n > 0:
                    q = 1 - b
                    dve.wait_ge(down_psum, j)
                    wait(dve, y_stored[q], 16 * (h + (b - 1) // 2))
                    nc.vector.tensor_copy(y_out[q], bank[3 + q][:, :]).then_inc(y_ready, 1)

            for n in range(2):
                expert(0, n, n)
            with dve.Fori(1, SLOT_TILES // 2) as h:
                for b in range(2):
                    expert(h, b, None)
            for n in range(SLOT_TILES - 1, SLOT_TILES + 1):
                expert(n // 2, n % 2, n)

            def add_results(g):
                for u in range(GT):
                    t = g * GT + u
                    dst = tile_of(resid, t)
                    for k in range(CHOICES):
                        buf = (u * CHOICES + k) % YBUFS
                        turn = g * (GT * CHOICES // YBUFS) + (u * CHOICES + k) // YBUFS
                        dve.wait_ge(y_gathered[buf], 16 * (turn + 1))
                        last = tt(dst, dst, y_in[buf], ALU.add)
                        if k == 0:
                            last.then_inc(y_half_added, 1)
                            dve.wait_ge(y_half_added, t + 1)
                        else:
                            last.then_inc(y_added, 1)

            add_results(0)
            with dve.Fori(1, GROUPS) as g:
                shared_multiply(g)
                add_results(g)
                dve.wait_ge(y_added, (g + 1) * GT)
                shared_add(g)

        @block.gpsimd
        def _(pool):
            def root(which, p):
                pool.wait_ge(meanvar_ready[which], p + 1)
                nc.gpsimd.tensor_tensor(veps[which][:, :], meanvar[which][:, 1:2], C["eps"], ALU.add).then_inc(veps_ready[which], 1)
                pool.wait_ge(veps_ready[which], p + 1)
                nc.gpsimd.tensor_tensor(rstd[which][:, :], veps[which][:, :], C["minus_half"], ALU.pow).then_inc(rstd_ready[which], 1)

            def iteration(h, b, n):
                if live(n, 1):
                    p, _ = pair(h, b, 1)
                    root(0, p)
                if live(n, 0):
                    p, _ = pair(h, b, 0)
                    pool.wait_ge(masked, p + 1)
                    pool.wait_ge(top_r_ready, p + 1)
                    w = segs(lagw)
                    nc.gpsimd.tensor_tensor(w, w, top_r[:, :].unsqueeze(2).to_broadcast([P, SEGS, L]),
                                            ALU.mult).then_inc(lagw_ready, 1)
                if live(n, -1):
                    p, _ = pair(h, b, -1)
                    root(1, p)
                if live(n, -2):
                    p, pb = pair(h, b, -2)
                    pool.wait_ge(x2T_ready, p + 1)
                    nc.gpsimd.tensor_copy(tile_of(x2T, p), x2T_tile[pb]).then_inc(x2T_kept, 1)

            pool.wait_ge(const_loaded, 16)
            root(0, 0)
            run(pool, iteration)

            def gather(h, b):
                j = 2 * h + b
                wait(pool, gathered[b], 16 * h)
                nc.gpsimd.tensor_copy(gidx[b][:, :], slot_token[:, bass.ds(j, 1)]).then_inc(gidx_ready, 1)
                wait(pool, xgT_psum, j - 1)
                pool.wait_ge(gidx_ready, j + 1)
                apart(pool, pool_passed)
                nc.gpsimd.indirect_dma_start(xg[b], None, x2_rows[:, :],
                                             bass.IndirectOffsetOnAxis(ap=gidx[b][:, 0:1], axis=0)).then_inc(gathered[b], 16)

            pool.wait_ge(slots_ready, 1)
            for b in range(2):
                pool.wait_ge(x2_stored[b], 16 * PAIRS // 2)
                gather(0, b)
            with pool.Fori(1, SLOT_TILES // 2) as h:
                for b in range(2):
                    gather(h, b)
            gather(SLOT_TILES // 2, 0)

            pool.wait_ge(y_stored[0], 16 * ((SLOT_TILES + 1) // 2))
            pool.wait_ge(y_stored[1], 16 * (SLOT_TILES // 2))
            pool.wait_ge(pos_ready, 1)
            pool.wait_ge(gathered[0], 16 * ((SLOT_TILES + 1) // 2))
            pool.wait_ge(gathered[1], 16 * (SLOT_TILES // 2))
            pos = pos_i[:, :].rearrange("p (k t) -> p k t", k=CHOICES)

            def gather_results(turn, first=False):
                for buf in range(YBUFS):
                    u, k = buf // CHOICES, buf % CHOICES
                    t = turn * (YBUFS // CHOICES) + u
                    wait(pool, y_gathered[buf], 16 * turn)
                    nc.gpsimd.tensor_copy(gidx[buf][:, :], pos[:, k, bass.ds(t, 1)]).then_inc(yidx_ready, 1)
                    pool.wait_ge(yidx_ready, turn * YBUFS + buf + 1)
                    if not first:
                        pool.wait_ge(y_added, t - 1)
                    apart(pool, pool_passed)
                    nc.gpsimd.indirect_dma_start(y_in[buf], None, y_rows[:, :],
                                                 bass.IndirectOffsetOnAxis(ap=gidx[buf][:, 0:1], axis=0)).then_inc(y_gathered[buf], 16)

            gather_results(0, first=True)
            with pool.Fori(1, PAIRS * CHOICES // YBUFS) as turn:
                gather_results(turn)


def kernel(x, ctx_4096, L0_ffn_gate_w, L0_ffn_w_gate_up, L0_ffn_w_down, L0_ffn_shared_w_gate_up, L0_ffn_shared_w_down):
    import concourse.bacc as bacc
    from concourse.bass_utils import run_bass_kernel_spmd

    def blocks(w):
        w = np.asarray(w)
        return np.ascontiguousarray(w.reshape(w.shape[0], w.shape[1] // P, P).transpose(2, 1, 0)).reshape(P, -1)

    gu = np.asarray(L0_ffn_w_gate_up)
    arrays = {
        "x": np.ascontiguousarray(x).reshape(TOKENS, D),
        "ctx": np.ascontiguousarray(ctx_4096).reshape(TOKENS, D),
        "consts": constants(),
        "gate": blocks(L0_ffn_gate_w),
        "w_gu": np.ascontiguousarray(gu.reshape(E, 2 * INTER, KB, P).transpose(3, 0, 2, 1)).reshape(P, -1),
        "w_down": np.ascontiguousarray(np.asarray(L0_ffn_w_down).transpose(2, 0, 1)).reshape(P, -1),
        "sh_gu": blocks(L0_ffn_shared_w_gate_up),
        "sh_down": blocks(L0_ffn_shared_w_down),
    }
    nc = bacc.Bacc("TRN2", target_bir_lowering=False, num_devices=1)
    args = [nc.dram_tensor(n, a.shape, F32, kind="ExternalInput").ap() for n, a in arrays.items()]
    out = nc.dram_tensor("result", (TOKENS, D), F32, kind="ExternalOutput").ap()
    build(nc, *args, out)
    result = run_bass_kernel_spmd(nc, [arrays], core_ids=[0]).results[0]["result"]
    return result.reshape(SEQS, L, D)
```

```python
from contextlib import ExitStack

import numpy as np

import concourse.bass as bass
from concourse import mybir

F32 = mybir.dt.float32
I32 = mybir.dt.int32
U32 = mybir.dt.uint32
ALU = mybir.AluOpType
ACT = mybir.ActivationFunctionType
AX = mybir.AxisListType

P = 128
SEQS, L, D = 32, 64, 512
TOKENS = SEQS * L
PAIRS = TOKENS // P
KB = D // P
TOPK = 8
SEGS = 2 * KB
E = 16
INTER = 128
SHARED = 512
SB = SHARED // P
CHOICES = 2
SLOT_TILES = (CHOICES * TOKENS + E * (P - 1)) // P
JW = SLOT_TILES + 1
GROUPS = 4
GT = PAIRS // GROUPS
EPS = 1e-5
TAKEN = -3.0e38
YBUFS = 4
HOTS = 4
HOT_TURNS = CHOICES * PAIRS // HOTS


def spectrum_rows(seq, real):
    return seq * 32 + np.arange(32) + (0 if real else 64)


def forward(odd, context):
    t, r = np.arange(L)[:, None], np.arange(32)[None, :]
    angle = np.pi * (2 * r + odd) * t / L
    re, im = np.cos(angle), -np.sin(angle)
    if not odd:
        im[:, 0] = (-1.0) ** t[:, 0]
    if context and odd:
        re[-1] -= re.sum(0)
        im[-1] -= im.sum(0)
    if context and not odd:
        re[-1, 0] += L
    out = np.zeros((P, P))
    for s in range(2):
        out[s * L:(s + 1) * L, spectrum_rows(s, True)] = re
        out[s * L:(s + 1) * L, spectrum_rows(s, False)] = im
    return out


def inverse(odd, swapped, sign, scale):
    t, r = np.arange(L)[None, :], np.arange(32)[:, None]
    angle = np.pi * (2 * r + odd) * t / L
    if swapped:
        re = sign * 2 * np.sin(angle) / L
        im = -re
        if not odd:
            re[0], im[0] = 0.0, 0.0
    else:
        re = 2 * np.cos(angle) / L
        im = re.copy()
        if not odd:
            re[0], im[0] = 1 / L, (-1.0) ** t[0] / L
    out = np.zeros((P, P))
    for s in range(2):
        out[spectrum_rows(s, True), s * L:(s + 1) * L] = re * scale
        out[spectrum_rows(s, False), s * L:(s + 1) * L] = im * scale
    return out


CONSTANTS = [
    ("even", P), ("even_context", P), ("odd", P), ("odd_context", P),
    ("corr_plain", P), ("corr_swapped", P),
    ("out_even_plain", P), ("out_even_swapped", P), ("out_odd_plain", P), ("out_odd_swapped", P),
    ("identity", P), ("earlier", P), ("ones", P), ("count", P), ("tile_edge", E),
    ("token", PAIRS), ("minus_half", 1), ("eps", 1), ("minus_one", 1),
]


def constants():
    p = np.arange(P)
    values = {
        "even": forward(0, False), "even_context": forward(0, True),
        "odd": forward(1, False), "odd_context": forward(1, True),
        "corr_plain": inverse(0, False, 1, 1.0), "corr_swapped": inverse(0, True, 1, 1.0),
        "out_even_plain": inverse(0, False, 1, 0.5), "out_even_swapped": inverse(0, True, -1, 0.5),
        "out_odd_plain": inverse(1, False, 1, 0.5), "out_odd_swapped": inverse(1, True, -1, 0.5),
        "identity": np.eye(P), "earlier": np.triu(np.ones((P, P)), 1), "ones": np.ones((P, P)),
        "count": np.tile(p, (P, 1)), "tile_edge": np.tile(P * np.arange(E), (P, 1)),
        "token": p[:, None] + P * np.arange(PAIRS)[None, :], "minus_half": np.full((P, 1), -0.5), "eps": np.full((P, 1), EPS),
        "minus_one": np.full((P, 1), -1.0),
    }
    return np.concatenate([values[n].astype(np.float32) for n, _ in CONSTANTS], axis=1)


def build(nc, x, ctx, consts, gate, w_gu, w_down, sh_gu, sh_down, out):
    with ExitStack() as stack:
        def sb(name, shape, dt=F32):
            return stack.enter_context(nc.sbuf_tensor(name, shape, dt))

        sems = {}

        def sem(name):
            sems[name] = stack.enter_context(nc.semaphore(name))
            return sems[name]

        def wait(eng, s, value):
            if not (isinstance(value, int) and value <= 0):
                eng.wait_ge(s, value)

        def apart(eng, passed):
            eng.sem_inc(passed, 1)

        x2_rows = nc.dram_tensor("x2_rows", [TOKENS, D], F32, kind="Internal").ap()
        y_rows = nc.dram_tensor("y_rows", [SLOT_TILES * P, D], F32, kind="Internal").ap()

        const_sb = sb("const_sb", [P, consts.shape[1]])
        at, C = 0, {}
        for name, width in CONSTANTS:
            C[name] = const_sb[:, at:at + width]
            at += width
        resid = sb("resid", [P, PAIRS * D])
        x2T = sb("x2T", [P, PAIRS * KB * P])
        wgu_sb = sb("wgu_sb", [P, E * KB * 2 * INTER])
        shgu_sb = sb("shgu_sb", [P, KB * 2 * SHARED])
        gate_sb = sb("gate_sb", [P, KB * E])
        arena = sb("arena", [P, 21 * D])
        xg_sb = sb("xg_sb", [P, 2 * D])
        silu_sb = sb("silu_sb", [P, D])
        b_at = [0]

        def cut():
            b_at[0] += 1
            return arena[:, (b_at[0] - 1) * D:b_at[0] * D]

        ctx_in = [cut(), cut()]
        xn = silu_sb[:, :]
        ctx_even, ctx_even_sw = [cut(), cut()], [cut(), cut()]
        ctx_odd, ctx_odd_sw = [cut(), cut()], [cut(), cut()]
        prod_plain, prod_swapped = cut(), cut()
        expz, lagw, lagwT = cut(), cut(), cut()
        out_prod = [cut() for _ in range(4)]
        x2n = [cut(), cut()]
        x2T_tile = [xg_sb[:, 0:D], xg_sb[:, D:2 * D]]
        assert b_at[0] == 21
        wd_sb = arena[:, 0:E * D]
        shd_sb = arena[:, E * D:(E + SB) * D]
        totals = arena[:, (E + SB) * D:(E + SB) * D + E * PAIRS]
        cumul = arena[:, (E + SB) * D + E * PAIRS:(E + SB + 1) * D]
        LAST_GU = (E // 2 - 1) * 2 * KB * 2 * INTER
        sh_act = wgu_sb[:, LAST_GU:LAST_GU + SB * D]
        xgT = [x2T[:, 0:D], x2T[:, D:2 * D]]
        y_out = [x2T[:, 2 * D:3 * D], x2T[:, 3 * D:4 * D]]
        xg = [xg_sb[:, 0:D], xg_sb[:, D:2 * D]]
        act_sb = sb("act_sb", [P, P])
        actT_both = sb("actT_both", [P, 2 * P])
        actT_sb = [actT_both[:, 0:P], actT_both[:, P:2 * P]]
        y_in = [wgu_sb[:, i * D:(i + 1) * D] for i in range(YBUFS)]

        stats = [sb(f"stats{i}", [P, 6]) for i in range(2)]
        meanvar = [sb(f"meanvar{i}", [P, 2]) for i in range(2)]
        rstd = [sb(f"rstd{i}", [P, 1]) for i in range(2)]
        veps = [sb(f"veps{i}", [P, 1]) for i in range(2)]
        negmean = [sb(f"negmean{i}", [P, 1]) for i in range(2)]
        shift = [sb(f"shift{i}", [P, 1]) for i in range(2)]
        top_v = sb("top_v", [P, SEGS * TOPK])
        top_e = sb("top_e", [P, SEGS * TOPK])
        top_s = sb("top_s", [P, SEGS])
        top_r = sb("top_r", [P, SEGS])
        logits = sb("logits", [P, PAIRS * E])
        r_val = sb("r_val", [P, PAIRS * 8])
        r_idx = sb("r_idx", [P, PAIRS * 8], U32)
        r_idxf = sb("r_idxf", [P, CHOICES * PAIRS])
        r_exp = sb("r_exp", [P, PAIRS])
        r_sum = sb("r_sum", [P, PAIRS])
        r_w = sb("r_w", [P, CHOICES * PAIRS])
        chosen = [xg_sb[:, k * PAIRS * E:(k + 1) * PAIRS * E] for k in range(CHOICES)]
        chosen_any = xg_sb[:, 2 * PAIRS * E:3 * PAIRS * E]
        route_tmp = xg_sb[:, 3 * PAIRS * E:4 * PAIRS * E]
        e_before = sb("e_before", [P, E])
        e_count = sb("e_count", [P, E])
        e_tiles = sb("e_tiles", [P, E])
        e_cum = sb("e_cum", [P, E])
        e_start = sb("e_start", [P, E])
        pos_f = sb("pos_f", [P, CHOICES * PAIRS])
        pos_i = sb("pos_i", [P, CHOICES * PAIRS], I32)
        hilo_i = sb("hilo_i", [P, CHOICES * PAIRS], I32)
        hi_f = sb("hi_f", [P, CHOICES * PAIRS])
        lo_f = sb("lo_f", [P, CHOICES * PAIRS])
        tile_e = sb("tile_e", [P, JW])
        tile_ei = sb("tile_ei", [P, JW], I32)
        lane_hot = [xg_sb[:, k * P:(k + 1) * P] for k in range(HOTS)]
        tile_hot = [xg_sb[:, HOTS * P + k * 2 * JW:HOTS * P + (k + 1) * 2 * JW] for k in range(HOTS)]
        slot_token = sb("slot_token", [P, JW], I32)
        slot_w = sb("slot_w", [P, JW])
        gidx = [sb(f"gidx{i}", [P, 1], I32) for i in range(YBUFS)]

        bank = [stack.enter_context(nc.psum_tensor(f"bank{i}", [P, D], F32)) for i in range(8)]
        ps_x, ps_even, ps_odd, ps_corr, ps_T, ps_w_even, ps_w_odd, ps_out = bank
        ps_xgT, ps_gu, ps_y, ps_actT = bank[0], bank[1:3], bank[3:5], bank[5]
        ps_gate, ps_up, ps_shared = bank[6], bank[7], (bank[0], bank[5])
        ps_slots, ps_rank, ps_total = bank[2], bank[3], bank[4]

        const_loaded = sem("const_loaded")
        x_loaded, ctx_loaded = [sem("x_loaded0"), sem("x_loaded1")], [sem("ctx_loaded0"), sem("ctx_loaded1")]
        gate_loaded, wgu_loaded, shgu_loaded = sem("gate_loaded"), sem("wgu_loaded"), sem("shgu_loaded")
        wd_loaded, shd_loaded = sem("wd_loaded"), sem("shd_loaded")
        x2_stored = [sem("x2_stored0"), sem("x2_stored1")]
        stats_done = [sem("x_stats_done"), sem("resid_stats_done")]
        meanvar_ready = [sem("x_meanvar_ready"), sem("resid_meanvar_ready")]
        veps_ready = [sem("x_veps_ready"), sem("resid_veps_ready")]
        root_ready = [sem("x_root_ready"), sem("resid_root_ready")]
        rstd_ready = [sem("x_rstd_ready"), sem("resid_rstd_ready")]
        xn_ready, x_spectrum = sem("xn_ready"), sem("x_spectrum")
        ctx_even_psum, ctx_even_ready = sem("ctx_even_psum"), sem("ctx_even_ready")
        ctx_odd_psum, ctx_odd_ready = sem("ctx_odd_psum"), sem("ctx_odd_ready")
        products_ready, corr_psum = sem("products_ready"), sem("corr_psum")
        maxima_ready, centered, lags_marked = sem("maxima_ready"), sem("centered"), sem("lags_marked")
        exp_ready, top_sum_ready, masked = sem("exp_ready"), sem("top_sum_ready"), sem("masked")
        top_r_ready = sem("top_r_ready")
        lagw_ready, lagwT_psum, lagwT_ready = sem("lagw_ready"), sem("lagwT_psum"), sem("lagwT_ready")
        w_even_psum, w_odd_psum = sem("w_even_psum"), sem("w_odd_psum")
        out_products_ready, out_psum, resid_ready = sem("out_products_ready"), sem("out_psum"), sem("resid_ready")
        x2n_ready, x2T_psum, x2T_ready, x2T_kept = sem("x2n_ready"), sem("x2T_psum"), sem("x2T_ready"), sem("x2T_kept")
        logits_psum, logits_ready = sem("logits_psum"), sem("logits_ready")
        route_step, route_diff, route_exp = sem("route_step"), sem("route_diff"), sem("route_exp")
        chosen_ready, counts_psum = sem("chosen_ready"), sem("counts_psum")
        hot_ready, slots_psum, slots_ready = sem("hot_ready"), sem("slots_psum"), sem("slots_ready")
        tile_e_ready, pos_ready = sem("tile_e_ready"), sem("pos_ready")
        sh_gate_psum, sh_up_psum, sh_silu = sem("sh_gate_psum"), sem("sh_up_psum"), sem("sh_silu")
        sh_act_ready, sh_out_psum, sh_added = sem("sh_act_ready"), sem("sh_out_psum"), sem("sh_added")
        gidx_ready = sem("gidx_ready")
        gathered = [sem("gathered0"), sem("gathered1")]
        xgT_psum, xgT_ready, gu_psum, silu_ready = sem("xgT_psum"), sem("xgT_ready"), sem("gu_psum"), sem("silu_ready")
        act_ready, actT_psum, actT_ready = sem("act_ready"), sem("actT_psum"), sem("actT_ready")
        down_psum, y_ready = sem("down_psum"), sem("y_ready")
        y_stored = [sem("y_stored0"), sem("y_stored1")]
        y_gathered = [sem(f"y_gathered{i}") for i in range(YBUFS)]
        yidx_ready, y_half_added, y_added = sem("yidx_ready"), sem("y_half_added"), sem("y_added")
        out_stored = sem("out_stored")
        dve_passed, pool_passed = sem("dve_passed"), sem("pool_passed")

        def tile_of(tensor, p):
            return tensor[:, bass.ds(p * D, D)]

        def segs(ap):
            return ap.rearrange("p (s l) -> p s l", s=SEGS)

        def schedule(iteration):
            for i in range(-2, 4):
                iteration(i // 2, i % 2, i)
            return range(2, (PAIRS - 2) // 2), [(i // 2, i % 2, i) for i in range(PAIRS - 2, PAIRS + 2)]

        def live(n, d):
            return n is None or 0 <= n + d < PAIRS

        def pair(h, b, d):
            return 2 * h + (b + d), (b + d) % 2

        def half(h, b, d):
            return h + (b + d) // 2

        def run(eng, iteration):
            hs, last = schedule(iteration)
            with eng.Fori(hs.start, hs.stop) as h:
                for b in range(2):
                    iteration(h, b, None)
            for h, b, n in last:
                iteration(h, b, n)

        block = stack.enter_context(nc.Block())

        @block.sync
        def _(sp):
            def load_pair(h, b):
                p = 2 * h + b
                wait(sp, ctx_odd_psum, p - 1)
                wait(sp, stats_done[0], p - 1)
                sp.dma_start(tile_of(resid, p), x[bass.ds(p * P, P), :]).then_inc(x_loaded[b], 16)
                sp.dma_start(ctx_in[b], ctx[bass.ds(p * P, P), :]).then_inc(ctx_loaded[b], 16)

            def load_expert_pair(h):
                width = 2 * KB * 2 * INTER
                sp.dma_start(wgu_sb[:, bass.ds(h * width, width)],
                             w_gu[:, bass.ds(h * width, width)]).then_inc(wgu_loaded, 16)

            def iteration(h, b, n):
                if live(n, 2) and n != -2:
                    load_pair(h + 1, b)
                if live(n, -2):
                    p, pb = pair(h, b, -2)
                    sp.wait_ge(x2n_ready, p + 1)
                    sp.dma_start(x2_rows[bass.ds(p * P, P), :], x2n[pb]).then_inc(x2_stored[pb], 16)
                if n == 2:
                    sp.dma_start(shgu_sb[:, :], sh_gu[:, :]).then_inc(shgu_loaded, 16)
                if b == 1 and (n is None or n == 3):
                    sp.wait_ge(wgu_loaded, 16 * h)
                    load_expert_pair(h)

            sp.dma_start(tile_of(resid, 0), x[0:P, :]).then_inc(x_loaded[0], 16)
            sp.dma_start(const_sb[:, :], consts[:, :]).then_inc(const_loaded, 16)
            sp.dma_start(ctx_in[0], ctx[0:P, :]).then_inc(ctx_loaded[0], 16)
            sp.dma_start(gate_sb[:, :], gate[:, :]).then_inc(gate_loaded, 16)
            load_expert_pair(0)
            run(sp, iteration)
            sp.wait_ge(logits_psum, PAIRS)
            sp.wait_ge(x2T_kept, PAIRS)
            for b in range(2):
                sp.wait_ge(x2_stored[b], 16 * PAIRS // 2)
            sp.dma_start(shd_sb, sh_down[:, :]).then_inc(shd_loaded, 16)
            sp.dma_start(wd_sb, w_down[:, :]).then_inc(wd_loaded, 16)
            sp.wait_ge(sh_out_psum, GT)
            sp.wait_ge(wgu_loaded, 16 * (E // 2 - 1))
            load_expert_pair(E // 2 - 1)

            def store_y(h, b):
                j = 2 * h + b
                sp.wait_ge(y_ready, j + 1)
                sp.dma_start(y_rows[bass.ds(j * P, P), :], y_out[b]).then_inc(y_stored[b], 16)

            with sp.Fori(0, SLOT_TILES // 2) as h:
                for b in range(2):
                    store_y(h, b)
            store_y(SLOT_TILES // 2, 0)
            with sp.Fori(0, PAIRS) as t:
                sp.wait_ge(y_added, t + 1)
                sp.wait_ge(sh_added, t + 1)
                sp.dma_start(out[bass.ds(t * P, P), :], tile_of(resid, t)).then_inc(out_stored, 16)
            sp.wait_ge(out_stored, 16 * PAIRS)

        @block.tensor
        def _(pe):
            mm = nc.tensor.matmul

            def iteration(h, b, n):
                if live(n, 0):
                    p, _ = pair(h, b, 0)
                    pe.wait_ge(products_ready, p + 1)
                    wait(pe, lags_marked, p)
                    for c in range(KB):
                        cols = slice(c * P, (c + 1) * P)
                        mm(ps_corr[:, cols], prod_plain[:, cols], C["corr_plain"], start=True, stop=False)
                        last = mm(ps_corr[:, cols], prod_swapped[:, cols], C["corr_swapped"], start=False, stop=True)
                    last.then_inc(corr_psum, 1)
                if live(n, 1):
                    p, pb = pair(h, b, 1)
                    pe.wait_ge(ctx_loaded[pb], 16 * (half(h, b, 1) + 1))
                    wait(pe, ctx_even_ready, p)
                    mm(ps_even[:, :], C["even_context"], ctx_in[pb], start=True, stop=True).then_inc(ctx_even_psum, 1)
                    pe.wait_ge(xn_ready, p + 1)
                    wait(pe, products_ready, p)
                    mm(ps_x[:, :], C["even"], xn, start=True, stop=True).then_inc(x_spectrum, 1)
                    wait(pe, ctx_odd_ready, p)
                    mm(ps_odd[:, :], C["odd_context"], ctx_in[pb], start=True, stop=True).then_inc(ctx_odd_psum, 1)
                if live(n, -2):
                    p, pb = pair(h, b, -2)
                    pe.wait_ge(x2n_ready, p + 1)
                    wait(pe, lagwT_ready, p + 2 if n is None else min(n, PAIRS))
                    for c in range(KB):
                        cols = slice(c * P, (c + 1) * P)
                        last = nc.tensor.transpose(ps_T[:, cols], x2n[pb][:, cols], C["identity"])
                    last.then_inc(x2T_psum, 1)
                if live(n, -1):
                    p, _ = pair(h, b, -1)
                    wait(pe, resid_ready, p)
                    parts = ("out_even_plain", "out_even_swapped", "out_odd_plain", "out_odd_swapped")
                    for m, name in enumerate(parts):
                        if m % 2 == 0:
                            pe.wait_ge(out_products_ready, 2 * p + 1 + m // 2)
                        last = mm(ps_out[:, :], C[name], out_prod[m], start=m == 0, stop=m == len(parts) - 1)
                    last.then_inc(out_psum, 1)
                if live(n, -2):
                    p, pb = pair(h, b, -2)
                    pe.wait_ge(x2T_ready, p + 1)
                    for c in range(KB):
                        last = mm(ps_w_odd[:, 0:E], x2T_tile[pb][:, c * P:(c + 1) * P], gate_sb[:, c * E:(c + 1) * E],
                                  start=c == 0, stop=c == KB - 1)
                    last.then_inc(logits_psum, 1)
                if live(n, 0):
                    p, _ = pair(h, b, 0)
                    pe.wait_ge(lagw_ready, p + 1)
                    wait(pe, x2T_ready, p - 1)
                    for c in range(KB):
                        cols = slice(c * P, (c + 1) * P)
                        last = nc.tensor.transpose(ps_T[:, cols], lagw[:, cols], C["identity"])
                    last.then_inc(lagwT_psum, 1)
                    pe.wait_ge(lagwT_ready, p + 1)
                    mm(ps_w_even[:, :], C["even"], lagwT, start=True, stop=True).then_inc(w_even_psum, 1)
                    wait(pe, logits_ready, p - 1)
                    mm(ps_w_odd[:, :], C["odd"], lagwT, start=True, stop=True).then_inc(w_odd_psum, 1)

            def shared_tokens(g, c):
                cols = x2T[:, bass.ds(g * GT * D, GT * D)]
                return cols.rearrange("p (t c n) -> p c t n", t=GT, c=KB)[:, c]

            def shared_half(g, m, part):
                ps, done, read = ((ps_gate, sh_gate_psum, sh_silu), (ps_up, sh_up_psum, sh_act_ready))[part]
                wait(pe, read, g * SB + m)
                for c in range(KB):
                    col = c * 2 * SHARED + part * SHARED + m * P
                    last = mm(ps[:, :].rearrange("p (t n) -> p t n", t=GT), shgu_sb[:, col:col + P], shared_tokens(g, c),
                              start=c == 0, stop=c == KB - 1)
                last.then_inc(done, 1)

            def shared_down(g, t):
                if t == 0:
                    pe.wait_ge(sh_act_ready, (g + 1) * SB)
                wait(pe, sh_added, g * GT + t - 1)
                for m in range(SB):
                    last = mm(ps_shared[t % 2][:, :], sh_act[:, m * D + t * P:m * D + (t + 1) * P],
                              shd_sb[:, m * D:(m + 1) * D], start=m == 0, stop=m == SB - 1)
                last.then_inc(sh_out_psum, 1)

            pe.wait_ge(const_loaded, 16)
            pe.wait_ge(gate_loaded, 16)
            run(pe, iteration)

            pe.wait_ge(logits_ready, PAIRS)
            pe.wait_ge(resid_ready, PAIRS)
            pe.wait_ge(x2T_kept, PAIRS)
            pe.wait_ge(shgu_loaded, 16)
            shared_half(0, 0, 0)
            shared_half(0, 0, 1)
            pe.wait_ge(chosen_ready, 1)
            mm(ps_rank[:, 0:PAIRS * E], C["earlier"], chosen_any, start=True, stop=True)
            mm(ps_total[:, 0:PAIRS * E], C["ones"], chosen_any, start=True, stop=True).then_inc(counts_psum, 1)
            for s in range(HOT_TURNS):
                if s < 2 * (SB - 1):
                    shared_half(0, 1 + s // 2, s % 2)
                else:
                    pe.wait_ge(shd_loaded, 16)
                    shared_down(0, s - 2 * (SB - 1))
                for i in range(HOTS):
                    pe.wait_ge(hot_ready, s * HOTS + i + 1)
                    mm(ps_slots[:, 0:2 * JW], lane_hot[i], tile_hot[i],
                       start=s == 0 and i == 0, stop=True, skip_group_check=True).then_inc(slots_psum, 1)
            for t in range(HOT_TURNS - 2 * (SB - 1), GT):
                shared_down(0, t)

            def transposes(h, b):
                j = 2 * h + b
                pe.wait_ge(gathered[b], 16 * (h + 1))
                wait(pe, xgT_ready, j)
                for c in range(KB):
                    cols = slice(c * P, (c + 1) * P)
                    last = nc.tensor.transpose(ps_xgT[:, cols], xg[b][:, cols], C["identity"])
                last.then_inc(xgT_psum, 1)

            def expert_of(j):
                return pe.value_load(tile_ei[0:1, bass.ds(j, 1)], min_val=0, max_val=E - 1)

            def expert(h, b, n):
                j = 2 * h + b
                if n is None or n < SLOT_TILES:
                    e = expert_of(j)
                    pe.wait_ge(xgT_ready, j + 1)
                    wait(pe, act_ready, j - 1)
                    for c in range(KB):
                        last = mm(ps_gu[b][:, 0:2 * INTER], xgT[b][:, c * P:(c + 1) * P],
                                  wgu_sb[:, bass.ds(e * (KB * 2 * INTER) + c * 2 * INTER, 2 * INTER)],
                                  start=c == 0, stop=c == KB - 1)
                    last.then_inc(gu_psum, 1)
                if n is None or n + 1 < SLOT_TILES:
                    transposes(h + (b + 1) // 2, (b + 1) % 2)
                if n is None or 1 <= n <= SLOT_TILES:
                    pe.wait_ge(act_ready, j)
                    wait(pe, actT_ready, j - 1)
                    nc.tensor.transpose(ps_actT[:, 0:P], act_sb[:, :], C["identity"]).then_inc(actT_psum, 1)
                if n is None or n >= 2:
                    e = expert_of(j - 2)
                    pe.wait_ge(actT_ready, j - 1)
                    wait(pe, y_ready, j - 3 if n is None or n > 2 else 0)
                    mm(ps_y[b][:, :], actT_sb[b], wd_sb[:, bass.ds(e * D, D)], start=True, stop=True).then_inc(down_psum, 1)

            pe.wait_ge(tile_e_ready, 1)
            pe.wait_ge(slots_ready, 1)
            pe.wait_ge(sh_added, GT)
            transposes(0, 0)
            pe.wait_ge(wd_loaded, 16)
            pe.wait_ge(wgu_loaded, 16 * E // 2)
            for n in range(4):
                expert(n // 2, n % 2, n)
            with pe.Fori(2, SLOT_TILES // 2) as h:
                for b in range(2):
                    expert(h, b, None)
            for n in range(SLOT_TILES - 1, SLOT_TILES + 2):
                expert(n // 2, n % 2, n)

            pe.wait_ge(xgT_ready, SLOT_TILES)
            pe.wait_ge(actT_ready, SLOT_TILES)
            with pe.Fori(1, GROUPS) as g:
                for m in range(SB):
                    for part in range(2):
                        shared_half(g, m, part)
                for t in range(GT):
                    shared_down(g, t)

        @block.scalar
        def _(act):
            copy = nc.scalar.copy

            def normalise(which, dst, src, p, done):
                act.wait_ge(rstd_ready[which], p + 1)
                nc.scalar.activation(dst, src, ACT.Identity, bias=shift[which][:, :], scale=rstd[which][:, :]).then_inc(done, 1)

            def iteration(h, b, n):
                if live(n, 1):
                    p, pb = pair(h, b, 1)
                    act.wait_ge(ctx_even_psum, p + 1)
                    wait(act, out_products_ready, 2 * (p - 1))
                    copy(ctx_even[pb], ps_even[:, :])
                    copy(ctx_even_sw[pb][0:64, :], ps_even[64:128, :])
                    copy(ctx_even_sw[pb][64:128, :], ps_even[0:64, :]).then_inc(ctx_even_ready, 1)
                if live(n, 0):
                    p, _ = pair(h, b, 0)
                    act.wait_ge(centered, p + 1)
                    nc.scalar.activation(top_e[:, :], top_e[:, :], ACT.Exp)
                    nc.scalar.activation(expz, expz, ACT.Exp).then_inc(exp_ready, 1)
                if live(n, -2):
                    p, pb = pair(h, b, -2)
                    act.wait_ge(x2T_psum, p + 1)
                    wait(act, x2T_kept, p - 1)
                    wait(act, logits_psum, p - 1)
                    copy(x2T_tile[pb], ps_T[:, :]).then_inc(x2T_ready, 1)
                if live(n, 1):
                    p, pb = pair(h, b, 1)
                    act.wait_ge(ctx_odd_psum, p + 1)
                    copy(ctx_odd[pb], ps_odd[:, :])
                    copy(ctx_odd_sw[pb][0:64, :], ps_odd[64:128, :])
                    copy(ctx_odd_sw[pb][64:128, :], ps_odd[0:64, :]).then_inc(ctx_odd_ready, 1)
                if live(n, -2):
                    p, _ = pair(h, b, -2)
                    act.wait_ge(logits_psum, p + 1)
                    copy(logits[:, bass.ds(p * E, E)], ps_w_odd[:, 0:E]).then_inc(logits_ready, 1)
                if live(n, 0):
                    p, _ = pair(h, b, 0)
                    act.wait_ge(lagwT_psum, p + 1)
                    wait(act, w_odd_psum, p)
                    copy(lagwT, ps_T[:, :]).then_inc(lagwT_ready, 1)
                if live(n, 2):
                    p, _ = pair(h, b, 2)
                    wait(act, x_spectrum, p)
                    normalise(0, xn, tile_of(resid, p), p, xn_ready)
                if live(n, -1):
                    p, pb = pair(h, b, -1)
                    wait(act, x2T_psum, p - 1)
                    wait(act, x2_stored[pb], 16 * half(h, b, -1))
                    normalise(1, x2n[pb], tile_of(resid, p), p, x2n_ready)

            run(act, iteration)

            act.wait_ge(route_diff, 1)
            nc.scalar.activation(r_exp[:, :], r_exp[:, :], ACT.Exp).then_inc(route_exp, 1)

            def shared_silu(g):
                for m in range(SB):
                    n = g * SB + m
                    act.wait_ge(sh_gate_psum, n + 1)
                    wait(act, sh_act_ready, n)
                    nc.scalar.activation(silu_sb[:, :], ps_gate[:, :], ACT.Silu).then_inc(sh_silu, 1)

            shared_silu(0)

            def gathered_T(h, b):
                j = 2 * h + b
                act.wait_ge(xgT_psum, j + 1)
                wait(act, gu_psum, j - 1)
                copy(xgT[b], ps_xgT[:, :]).then_inc(xgT_ready, 1)

            def expert(h, b, n):
                j = 2 * h + b
                if n is None or n + 1 < SLOT_TILES:
                    gathered_T(h + (b + 1) // 2, (b + 1) % 2)
                act.wait_ge(gu_psum, j + 1)
                wait(act, act_ready, j)
                nc.scalar.activation(silu_sb[:, 0:INTER], ps_gu[b][:, 0:INTER], ACT.Silu).then_inc(silu_ready, 1)

            act.wait_ge(sh_out_psum, GT)
            gathered_T(0, 0)
            for n in range(2):
                expert(0, n, n)
            with act.Fori(1, SLOT_TILES // 2) as h:
                for b in range(2):
                    expert(h, b, None)
            expert(SLOT_TILES // 2, 0, SLOT_TILES - 1)

            with act.Fori(1, GROUPS) as g:
                shared_silu(g)

        @block.vector
        def _(dve):
            tt, ts, stt = nc.vector.tensor_tensor, nc.vector.tensor_scalar, nc.vector.scalar_tensor_tensor

            def moments(which, src, p):
                nc.vector.bn_stats(stats[which][:, :], src).then_inc(stats_done[which], 1)
                dve.wait_ge(stats_done[which], p + 1)
                apart(dve, dve_passed)
                nc.vector.bn_aggr(meanvar[which][:, :], stats[which][:, :]).then_inc(meanvar_ready[which], 1)

            def iteration(h, b, n):
                if live(n, -1):
                    p, pb = pair(h, b, -1)
                    dve.wait_ge(w_even_psum, p + 1)
                    tt(out_prod[0], ps_w_even[:, :], ctx_even[pb], ALU.mult)
                    tt(out_prod[1], ps_w_even[:, :], ctx_even_sw[pb], ALU.mult).then_inc(out_products_ready, 1)
                    dve.wait_ge(w_odd_psum, p + 1)
                    dve.wait_ge(ctx_odd_ready, p + 1)
                    tt(out_prod[2], ps_w_odd[:, :], ctx_odd[pb], ALU.mult)
                    tt(out_prod[3], ps_w_odd[:, :], ctx_odd_sw[pb], ALU.mult).then_inc(out_products_ready, 1)
                if live(n, 0):
                    p, _ = pair(h, b, 0)
                    dve.wait_ge(corr_psum, p + 1)
                    apart(dve, dve_passed)
                    lags, tops = segs(ps_corr[:, :]), segs(top_v[:, :])
                    for s in range(SEGS):
                        last = nc.vector.max(tops[:, s], lags[:, s])
                    last.then_inc(maxima_ready, 1)
                    dve.wait_ge(maxima_ready, p + 1)
                    largest = tops[:, :, 0:1]
                    tt(segs(top_e[:, :]), tops, largest.to_broadcast([P, SEGS, TOPK]), ALU.subtract)
                    tt(segs(expz), lags, largest.to_broadcast([P, SEGS, L]), ALU.subtract).then_inc(centered, 1)
                    for s in range(SEGS):
                        last = nc.vector.match_replace(segs(lagw)[:, s], tops[:, s], lags[:, s], TAKEN)
                    last.then_inc(lags_marked, 1)
                    dve.wait_ge(exp_ready, p + 1)
                    nc.vector.reduce_sum(top_s[:, :], segs(top_e[:, :]), axis=AX.X).then_inc(top_sum_ready, 1)
                    dve.wait_ge(lags_marked, p + 1)
                    stt(lagw, lagw, TAKEN, expz, ALU.is_equal, ALU.mult).then_inc(masked, 1)
                    dve.wait_ge(top_sum_ready, p + 1)
                    nc.vector.reciprocal(top_r[:, :], top_s[:, :]).then_inc(top_r_ready, 1)
                if live(n, 1):
                    p, pb = pair(h, b, 1)
                    dve.wait_ge(x_spectrum, p + 1)
                    dve.wait_ge(ctx_even_ready, p + 1)
                    tt(prod_plain, ps_x[:, :], ctx_even[pb], ALU.mult)
                    tt(prod_swapped, ps_x[:, :], ctx_even_sw[pb], ALU.mult).then_inc(products_ready, 1)
                if live(n, 2):
                    p, pb = pair(h, b, 2)
                    wait(dve, xn_ready, p)
                    dve.wait_ge(x_loaded[pb], 16 * (half(h, b, 2) + 1))
                    apart(dve, dve_passed)
                    moments(0, tile_of(resid, p), p)
                if live(n, -1):
                    p, pb = pair(h, b, -1)
                    dve.wait_ge(out_psum, p + 1)
                    tt(tile_of(resid, p), ps_out[:, :], tile_of(resid, p), ALU.add).then_inc(resid_ready, 1)
                    dve.wait_ge(resid_ready, p + 1)
                    apart(dve, dve_passed)
                    moments(1, tile_of(resid, p), p)

            dve.wait_ge(const_loaded, 16)
            run(dve, iteration)

            steps = [0]

            def then(ins):
                steps[0] += 1
                ins.then_inc(route_step, 1)
                dve.wait_ge(route_step, steps[0])

            def by_expert(ap):
                return ap.rearrange("p (t e) -> p t e", e=E)

            def expert_major(ap):
                return ap.rearrange("p (e t) -> p e t", e=E)

            def over(ap, dims, axis):
                return ap.unsqueeze(axis).to_broadcast(dims)

            dve.wait_ge(logits_ready, PAIRS)
            dve.wait_ge(x2T_kept, PAIRS)
            vals, idx = r_val[:, :].rearrange("p (t v) -> p t v", v=8), r_idx[:, :].rearrange("p (t v) -> p t v", v=8)
            log_t = by_expert(logits[:, :])
            for t in range(PAIRS):
                last = nc.vector.max(vals[:, t], log_t[:, t])
            then(last)
            for t in range(PAIRS):
                last = nc.vector.max_index(idx[:, t], vals[:, t], log_t[:, t])
            tt(r_exp[:, :], vals[:, :, 1], vals[:, :, 0], ALU.subtract).then_inc(route_diff, 1)
            then(last)
            idxf = r_idxf[:, :].rearrange("p (k t) -> p k t", k=CHOICES)
            then(nc.vector.tensor_copy(idxf, idx[:, :, 0:CHOICES].rearrange("p t k -> p k t")))
            dims = [P, PAIRS, E]
            for k in range(CHOICES):
                last = tt(by_expert(chosen[k]), over(C["count"][:, 0:E], dims, 1), over(idxf[:, k], dims, 2), ALU.is_equal)
            then(last)
            tt(chosen_any, chosen[0], chosen[1], ALU.add).then_inc(chosen_ready, 1)
            wts = r_w[:, :].rearrange("p (k t) -> p k t", k=CHOICES)
            dve.wait_ge(route_exp, 1)
            then(ts(r_sum[:, :], r_exp[:, :], 1.0, None, ALU.add))
            then(nc.vector.reciprocal(wts[:, 0], r_sum[:, :]))
            then(tt(wts[:, 1], r_exp[:, :], wts[:, 0], ALU.mult))

            def shared_multiply(g, m):
                dve.wait_ge(sh_silu, g * SB + m + 1)
                dve.wait_ge(sh_up_psum, g * SB + m + 1)
                if m == 0:
                    wait(dve, sh_out_psum, g * GT)
                tt(sh_act[:, m * D:(m + 1) * D], ps_up[:, :], silu_sb[:, :], ALU.mult).then_inc(sh_act_ready, 1)

            def shared_add(g, t):
                dve.wait_ge(sh_out_psum, g * GT + t + 1)
                dst = tile_of(resid, g * GT + t)
                tt(dst, ps_shared[t % 2][:, :], dst, ALU.add).then_inc(sh_added, 1)

            dve.wait_ge(shd_loaded, 16)
            shared_multiply(0, 0)
            dve.wait_ge(counts_psum, 1)
            totals3, cumul3 = expert_major(totals), expert_major(cumul)
            then(nc.vector.tensor_copy(totals3, by_expert(ps_total[:, 0:PAIRS * E]).rearrange("p t e -> p e t")))
            then(nc.vector.tensor_tensor_scan(cumul, C["ones"][:, 0:1].to_broadcast([P, E * PAIRS]), totals, 0.0, ALU.mult, ALU.add))
            nc.vector.memset(e_before[:, 0:1], 0.0)
            then(nc.vector.tensor_copy(e_before[:, 1:E], cumul3[:, 0:E - 1, PAIRS - 1]))
            then(tt(e_count[:, :], cumul3[:, :, PAIRS - 1], e_before[:, :], ALU.subtract))
            edges = expert_major(route_tmp)
            then(tt(edges, over(e_count[:, :], [P, E, E], 2), over(C["tile_edge"], [P, E, E], 1), ALU.is_gt))
            then(nc.vector.reduce_sum(e_tiles[:, :], edges, axis=AX.X))
            then(nc.vector.tensor_tensor_scan(e_cum[:, :], C["ones"][:, 0:E], e_tiles[:, :], 0.0, ALU.mult, ALU.add))
            then(tt(e_start[:, :], e_cum[:, :], e_tiles[:, :], ALU.subtract))
            then(stt(e_start[:, :], e_start[:, :], float(P), e_before[:, :], ALU.mult, ALU.subtract))
            then(tt(cumul, cumul, totals, ALU.subtract))
            then(tt(cumul3, cumul3, over(e_start[:, :], [P, E, PAIRS], 2), ALU.add))
            then(tt(by_expert(totals), by_expert(ps_rank[:, 0:PAIRS * E]), cumul3.rearrange("p e t -> p t e"), ALU.add))
            pos = pos_f[:, :].rearrange("p (k t) -> p k t", k=CHOICES)
            for k in range(CHOICES):
                then(tt(route_tmp, chosen[k], totals, ALU.mult))
                then(nc.vector.reduce_sum(pos[:, k], by_expert(route_tmp), axis=AX.X))
            nc.vector.tensor_copy(pos_i[:, :], pos_f[:, :]).then_inc(pos_ready, 1)
            dve.wait_ge(pos_ready, 1)
            then(nc.vector.tensor_scalar(hilo_i[:, :], pos_i[:, :], 7, None, ALU.logical_shift_right))
            then(nc.vector.tensor_copy(hi_f[:, :], hilo_i[:, :]))
            then(nc.vector.tensor_scalar(hilo_i[:, :], pos_i[:, :], P - 1, None, ALU.bitwise_and))
            then(nc.vector.tensor_copy(lo_f[:, :], hilo_i[:, :]))
            step = PAIRS
            for j in range(0, JW, step):
                ended = route_tmp.rearrange("p (j e) -> p j e", e=E)
                then(tt(ended, over(e_cum[:, :], [P, step, E], 1), over(C["count"][:, j:j + step], [P, step, E], 2), ALU.is_le))
                then(nc.vector.reduce_sum(tile_e[:, j:j + step], ended, axis=AX.X))
            then(nc.vector.tensor_scalar(tile_e[:, :], tile_e[:, :], float(E - 1), None, ALU.min))
            nc.vector.tensor_copy(tile_ei[:, :], tile_e[:, :]).then_inc(tile_e_ready, 1)

            hi, lo = hi_f[:, :].rearrange("p (k t) -> p k t", k=CHOICES), lo_f[:, :].rearrange("p (k t) -> p k t", k=CHOICES)

            for s in range(HOT_TURNS):
                for i in range(HOTS):
                    t, k = divmod(s * HOTS + i, CHOICES)
                    wait(dve, slots_psum, (s - 1) * HOTS + i + 1)
                    ts(lane_hot[i], C["count"], lo[:, k, t:t + 1], None, ALU.is_equal)
                    ts(tile_hot[i][:, 0:JW], C["count"][:, 0:JW], hi[:, k, t:t + 1],
                       C["token"][:, t:t + 1], ALU.is_equal, ALU.mult)
                    ts(tile_hot[i][:, JW:2 * JW], C["count"][:, 0:JW], hi[:, k, t:t + 1],
                       wts[:, k, t:t + 1], ALU.is_equal, ALU.mult).then_inc(hot_ready, 1)
                if s % 2 and s // 2 + 1 < SB:
                    shared_multiply(0, s // 2 + 1)
            dve.wait_ge(slots_psum, CHOICES * PAIRS)
            nc.vector.tensor_copy(slot_w[:, :], ps_slots[:, JW:2 * JW])
            nc.vector.tensor_copy(slot_token[:, :], ps_slots[:, 0:JW]).then_inc(slots_ready, 1)
            for t in range(GT):
                shared_add(0, t)
            dve.wait_ge(slots_ready, 1)

            def expert(h, b, n):
                j = 2 * h + b
                if n is None or 1 <= n <= SLOT_TILES:
                    dve.wait_ge(actT_psum, j)
                    wait(dve, down_psum, j - 2)
                    nc.vector.tensor_copy(actT_sb[1 - b], ps_actT[:, 0:P]).then_inc(actT_ready, 1)
                if n is None or n < SLOT_TILES:
                    dve.wait_ge(silu_ready, j + 1)
                    stt(act_sb[:, :], ps_gu[b][:, INTER:2 * INTER], slot_w[:, bass.ds(j, 1)], silu_sb[:, 0:INTER],
                        ALU.mult, ALU.mult).then_inc(act_ready, 1)
                if n is None or n >= 2:
                    dve.wait_ge(down_psum, j - 1)
                    wait(dve, y_stored[b], 16 * (h - 1))
                    nc.vector.tensor_copy(y_out[b], ps_y[b][:, :]).then_inc(y_ready, 1)

            for n in range(2):
                expert(0, n, n)
            with dve.Fori(1, SLOT_TILES // 2) as h:
                for b in range(2):
                    expert(h, b, None)
            for n in range(SLOT_TILES - 1, SLOT_TILES + 2):
                expert(n // 2, n % 2, n)

            def add_results(quad, u):
                t = quad * GT + u
                dst = tile_of(resid, t)
                for k in range(CHOICES):
                    buf = (u % 2) * CHOICES + k
                    dve.wait_ge(y_gathered[buf], 16 * (quad * 2 + u // 2 + 1))
                    if k == 0:
                        tt(dst, dst, y_in[buf], ALU.add).then_inc(y_half_added, 1)
                        dve.wait_ge(y_half_added, t + 1)
                    else:
                        tt(dst, dst, y_in[buf], ALU.add).then_inc(y_added, 1)

            def last_groups(g, last):
                for m in range(SB):
                    shared_multiply(g, m)
                    add_results(g - 1, m)
                for t in range(GT):
                    shared_add(g, t)
                    if last:
                        dve.wait_ge(sh_added, g * GT + t + 1)
                        add_results(g, t)

            with dve.Fori(1, GROUPS - 1) as g:
                last_groups(g, False)
            last_groups(GROUPS - 1, True)

        @block.gpsimd
        def _(pool):
            def root(which, p):
                tt = nc.gpsimd.tensor_tensor
                pool.wait_ge(meanvar_ready[which], p + 1)
                wait(pool, (xn_ready, x2n_ready)[which], p)
                tt(negmean[which][:, :], meanvar[which][:, 0:1], C["minus_one"], ALU.mult)
                tt(veps[which][:, :], meanvar[which][:, 1:2], C["eps"], ALU.add).then_inc(veps_ready[which], 1)
                pool.wait_ge(veps_ready[which], p + 1)
                tt(rstd[which][:, :], veps[which][:, :], C["minus_half"], ALU.pow).then_inc(root_ready[which], 1)
                pool.wait_ge(root_ready[which], p + 1)
                tt(shift[which][:, :], negmean[which][:, :], rstd[which][:, :], ALU.mult).then_inc(rstd_ready[which], 1)

            def iteration(h, b, n):
                if live(n, 0):
                    p, _ = pair(h, b, 0)
                    pool.wait_ge(masked, p + 1)
                    pool.wait_ge(top_r_ready, p + 1)
                    w = segs(lagw)
                    nc.gpsimd.tensor_tensor(w, w, top_r[:, :].unsqueeze(2).to_broadcast([P, SEGS, L]),
                                            ALU.mult).then_inc(lagw_ready, 1)
                if live(n, 2):
                    p, _ = pair(h, b, 2)
                    root(0, p)
                if live(n, -1):
                    p, _ = pair(h, b, -1)
                    root(1, p)
                if live(n, -2):
                    p, pb = pair(h, b, -2)
                    pool.wait_ge(x2T_ready, p + 1)
                    nc.gpsimd.tensor_copy(tile_of(x2T, p), x2T_tile[pb]).then_inc(x2T_kept, 1)

            pool.wait_ge(const_loaded, 16)
            run(pool, iteration)

            def gather(h, b):
                j = 2 * h + b
                wait(pool, gathered[b], 16 * h)
                nc.gpsimd.tensor_copy(gidx[b][:, :], slot_token[:, bass.ds(j, 1)]).then_inc(gidx_ready, 1)
                wait(pool, xgT_psum, j - 1)
                pool.wait_ge(gidx_ready, j + 1)
                apart(pool, pool_passed)
                nc.gpsimd.indirect_dma_start(xg[b], None, x2_rows[:, :],
                                             bass.IndirectOffsetOnAxis(ap=gidx[b][:, 0:1], axis=0)).then_inc(gathered[b], 16)

            pool.wait_ge(slots_ready, 1)
            for b in range(2):
                pool.wait_ge(x2_stored[b], 16 * PAIRS // 2)
                gather(0, b)
            with pool.Fori(1, SLOT_TILES // 2) as h:
                for b in range(2):
                    gather(h, b)
            gather(SLOT_TILES // 2, 0)

            pool.wait_ge(y_stored[0], 16 * ((SLOT_TILES + 1) // 2))
            pool.wait_ge(y_stored[1], 16 * (SLOT_TILES // 2))
            pool.wait_ge(pos_ready, 1)
            pool.wait_ge(gathered[0], 16 * ((SLOT_TILES + 1) // 2))
            pool.wait_ge(gathered[1], 16 * (SLOT_TILES // 2))
            pos = pos_i[:, :].rearrange("p (k t) -> p k t", k=CHOICES)

            def gather_results(turn, first=False):
                for buf in range(YBUFS):
                    u, k = buf // CHOICES, buf % CHOICES
                    t = turn * (YBUFS // CHOICES) + u
                    wait(pool, y_gathered[buf], 16 * turn)
                    nc.gpsimd.tensor_copy(gidx[buf][:, :], pos[:, k, bass.ds(t, 1)]).then_inc(yidx_ready, 1)
                    pool.wait_ge(yidx_ready, turn * YBUFS + buf + 1)
                    if not first:
                        pool.wait_ge(y_added, t - 1)
                    apart(pool, pool_passed)
                    nc.gpsimd.indirect_dma_start(y_in[buf], None, y_rows[:, :],
                                                 bass.IndirectOffsetOnAxis(ap=gidx[buf][:, 0:1], axis=0)).then_inc(y_gathered[buf], 16)

            gather_results(0, first=True)
            with pool.Fori(1, PAIRS * CHOICES // YBUFS) as turn:
                gather_results(turn)


def kernel(x, ctx_4096, L0_ffn_gate_w, L0_ffn_w_gate_up, L0_ffn_w_down, L0_ffn_shared_w_gate_up, L0_ffn_shared_w_down):
    import concourse.bacc as bacc
    from concourse.bass_utils import run_bass_kernel_spmd

    def blocks(w):
        w = np.asarray(w)
        return np.ascontiguousarray(w.reshape(w.shape[0], w.shape[1] // P, P).transpose(2, 1, 0)).reshape(P, -1)

    gu = np.asarray(L0_ffn_w_gate_up)
    arrays = {
        "x": np.ascontiguousarray(x).reshape(TOKENS, D),
        "ctx": np.ascontiguousarray(ctx_4096).reshape(TOKENS, D),
        "consts": constants(),
        "gate": blocks(L0_ffn_gate_w),
        "w_gu": np.ascontiguousarray(gu.reshape(E, 2 * INTER, KB, P).transpose(3, 0, 2, 1)).reshape(P, -1),
        "w_down": np.ascontiguousarray(np.asarray(L0_ffn_w_down).transpose(2, 0, 1)).reshape(P, -1),
        "sh_gu": blocks(L0_ffn_shared_w_gate_up),
        "sh_down": blocks(L0_ffn_shared_w_down),
    }
    nc = bacc.Bacc("TRN2", target_bir_lowering=False, num_devices=1)
    args = [nc.dram_tensor(n, a.shape, F32, kind="ExternalInput").ap() for n, a in arrays.items()]
    out = nc.dram_tensor("result", (TOKENS, D), F32, kind="ExternalOutput").ap()
    build(nc, *args, out)
    result = run_bass_kernel_spmd(nc, [arrays], core_ids=[0]).results[0]["result"]
    return result.reshape(SEQS, L, D)
```

```python
from contextlib import ExitStack

import numpy as np

import concourse.bass as bass
from concourse import mybir

F32 = mybir.dt.float32
F32R = mybir.dt.float32r
I32 = mybir.dt.int32
U32 = mybir.dt.uint32
ALU = mybir.AluOpType
ACT = mybir.ActivationFunctionType
AX = mybir.AxisListType

P = 128
SEQS, L, D = 32, 64, 512
TOKENS = SEQS * L
PAIRS = TOKENS // P
KB = D // P
TOPK = 8
SEGS = 2 * KB
E = 16
INTER = 128
SHARED = 512
SB = SHARED // P
CHOICES = 2
SLOT_TILES = (CHOICES * TOKENS + E * (P - 1)) // P
JW = SLOT_TILES + 1
GROUPS = 4
GT = PAIRS // GROUPS
EPS = 1e-5
TAKEN = -3.0e38
YTILES = 4
YBUFS = YTILES * CHOICES
HOTS = 4
HOT_TURNS = CHOICES * PAIRS // HOTS


def spectrum_rows(seq, real):
    return seq * 32 + np.arange(32) + (0 if real else 64)


def forward(odd, context):
    t, r = np.arange(L)[:, None], np.arange(32)[None, :]
    angle = np.pi * (2 * r + odd) * t / L
    re, im = np.cos(angle), -np.sin(angle)
    if not odd:
        im[:, 0] = (-1.0) ** t[:, 0]
    if context and odd:
        re[-1] -= re.sum(0)
        im[-1] -= im.sum(0)
    if context and not odd:
        re[-1, 0] += L
    out = np.zeros((P, P))
    for s in range(2):
        out[s * L:(s + 1) * L, spectrum_rows(s, True)] = re
        out[s * L:(s + 1) * L, spectrum_rows(s, False)] = im
    return out


def inverse_spectrum(odd, scale):
    t, r = np.arange(L)[None, :], np.arange(32)[:, None]
    angle = np.pi * (2 * r + odd) * t / L
    out = np.zeros((P, P))
    for s in range(2):
        out[spectrum_rows(s, True), s * L:(s + 1) * L] = 2 * np.cos(angle) / L * scale
        out[spectrum_rows(s, False), s * L:(s + 1) * L] = 2 * np.sin(angle) / L * scale
    return out


def inverse(odd, swapped, sign, scale):
    t, r = np.arange(L)[None, :], np.arange(32)[:, None]
    angle = np.pi * (2 * r + odd) * t / L
    if swapped:
        re = sign * 2 * np.sin(angle) / L
        im = -re
        if not odd:
            re[0], im[0] = 0.0, 0.0
    else:
        re = 2 * np.cos(angle) / L
        im = re.copy()
        if not odd:
            re[0], im[0] = 1 / L, (-1.0) ** t[0] / L
    out = np.zeros((P, P))
    for s in range(2):
        out[spectrum_rows(s, True), s * L:(s + 1) * L] = re * scale
        out[spectrum_rows(s, False), s * L:(s + 1) * L] = im * scale
    return out


CONSTANTS = [
    ("minus_half", 1), ("eps", 1), ("minus_one", 1),
    ("even", P), ("odd", P), ("context", 2 * P),
    ("corr_plain", P), ("corr_swapped", P),
    ("out_even_plain", P), ("out_even_swapped", P), ("out_odd", P),
    ("identity", P), ("earlier", P), ("ones", P), ("count", P), ("tile_edge", E),
    ("token", PAIRS),
]
EARLY = 3 + 4 * P


def constants():
    p = np.arange(P)
    values = {
        "even": forward(0, False), "odd": forward(1, False),
        "context": np.concatenate([forward(0, True), forward(1, True)], axis=1),
        "corr_plain": inverse(0, False, 1, 1.0), "corr_swapped": inverse(0, True, 1, 1.0),
        "out_even_plain": inverse(0, False, 1, 0.5), "out_even_swapped": inverse(0, True, -1, 0.5),
        "out_odd": inverse_spectrum(1, 0.5),
        "identity": np.eye(P), "earlier": np.triu(np.ones((P, P)), 1), "ones": np.ones((P, P)),
        "count": np.tile(p, (P, 1)), "tile_edge": np.tile(P * np.arange(E), (P, 1)),
        "token": p[:, None] + P * np.arange(PAIRS)[None, :],
        "minus_half": np.full((P, 1), -0.5), "eps": np.full((P, 1), EPS),
        "minus_one": np.full((P, 1), -1.0),
    }
    return np.concatenate([values[n].astype(np.float32) for n, _ in CONSTANTS], axis=1)


def build(nc, x, ctx, consts, gate, w_gu, w_down, sh_gu, sh_down, out):
    with ExitStack() as stack:
        def sb(name, shape, dt=F32):
            return stack.enter_context(nc.sbuf_tensor(name, shape, dt))

        def in_turn(name, width, later):
            with nc.sbuf_tensor(name, [P, width], F32) as first:
                pass
            spare = width - sum(w for _, w, _ in later)
            tenants = [sb(n, [P, w], dt) for n, w, dt in later]
            if spare:
                sb(name + "_spare", [P, spare])
            return first, tenants

        sems = {}

        def sem(name):
            sems[name] = stack.enter_context(nc.semaphore(name))
            return sems[name]

        def wait(eng, s, value):
            if not (isinstance(value, int) and value <= 0):
                eng.wait_ge(s, value)

        def apart(eng, passed):
            eng.sem_inc(passed, 1)

        x2_rows = nc.dram_tensor("x2_rows", [TOKENS, D], F32, kind="Internal").ap()
        y_rows = nc.dram_tensor("y_rows", [SLOT_TILES * P, D], F32, kind="Internal").ap()

        const_sb = sb("const_sb", [P, consts.shape[1]])
        at, C = 0, {}
        for name, width in CONSTANTS:
            C[name] = const_sb[:, at:at + width]
            at += width
        resid = sb("resid", [P, PAIRS * D])
        x2T = sb("x2T", [P, PAIRS * KB * P])
        wgu_sb, (y_in_low, shgu_hi, shgu_lo, tokens_hi, tokens_lo, act_lo) = in_turn("wgu_sb", E * KB * 2 * INTER, [
            ("y_in_low", YBUFS // 2 * D, F32), ("shgu_hi", KB * 2 * SHARED, F32R), ("shgu_lo", KB * 2 * SHARED, F32R),
            ("tokens_hi", GT * D, F32R), ("tokens_lo", GT * D, F32R), ("act_lo", SB * D, F32R)])
        shgu_sb = sb("shgu_sb", [P, KB * 2 * SHARED])
        gate_sb = sb("gate_sb", [P, KB * E])
        arena, (shd_hi, shd_lo, act_hi) = in_turn("arena", 21 * D, [
            ("shd_hi", SB * D, F32R), ("shd_lo", SB * D, F32R), ("act_hi", SB * D, F32R)])
        xg_sb = sb("xg_sb", [P, 2 * D])
        silu_sb = sb("silu_sb", [P, D])
        b_at = [0]

        def cut():
            b_at[0] += 1
            return arena[:, (b_at[0] - 1) * D:b_at[0] * D]

        ctx_halves = (act_lo[:, 0:D], act_lo[:, D:2 * D])
        matrices_halves = (act_lo[:, 2 * D:2 * D + 2 * P], act_lo[:, 2 * D + 2 * P:2 * D + 4 * P])
        ctx_in = [cut(), cut()]
        xn = silu_sb[:, :]
        ctx_even, ctx_even_sw = [cut(), cut()], [cut(), cut()]
        ctx_odd_re, ctx_odd_im = [cut(), cut()], [cut(), cut()]
        prod_plain, prod_swapped = cut(), cut()
        expz, lagw, lagwT = cut(), cut(), cut()
        out_prod = [cut(), cut()]
        odd_prod = cut()
        w_odd_sw = cut()
        x2n = [cut(), cut()]
        x2T_tile = [xg_sb[:, 0:D], xg_sb[:, D:2 * D]]
        assert b_at[0] == 21
        wd_sb = arena[:, 0:E * D]
        shd_sb = arena[:, E * D:(E + SB) * D]
        totals = arena[:, (E + SB) * D:(E + SB) * D + E * PAIRS]
        cumul = arena[:, (E + SB) * D + E * PAIRS:(E + SB + 1) * D]
        EARLY_DOWN = (E - SB) * D
        sh_act = arena[:, EARLY_DOWN:EARLY_DOWN + SB * D]
        assert SB * P == D and GT == SB

        def act_block(m):
            return sh_act.rearrange("p (t m n) -> p t m n", t=GT, m=SB)[:, :, m]

        xgT = [x2T[:, 0:D], x2T[:, D:2 * D]]
        y_out = [x2T[:, 2 * D:3 * D], x2T[:, 3 * D:4 * D]]
        xg = [xg_sb[:, 0:D], xg_sb[:, D:2 * D]]
        act_sb = sb("act_sb", [P, P])
        actT_both = sb("actT_both", [P, 2 * P])
        actT_sb = [actT_both[:, 0:P], actT_both[:, P:2 * P]]
        y_in = [(y_in_low if i < YBUFS // 2 else x2T)[:, i % (YBUFS // 2) * D:(i % (YBUFS // 2) + 1) * D] for i in range(YBUFS)]
        shgu_halves, shd_halves, act_halves = (shgu_hi, shgu_lo), (shd_hi, shd_lo), (act_hi, act_lo)
        tokens_halves = (tokens_hi, tokens_lo)

        stats = [sb(f"stats{i}", [P, 6]) for i in range(2)]
        meanvar = [sb(f"meanvar{i}", [P, 2]) for i in range(2)]
        rstd = [sb(f"rstd{i}", [P, 1]) for i in range(2)]
        veps = [sb(f"veps{i}", [P, 1]) for i in range(2)]
        negmean = [sb(f"negmean{i}", [P, 1]) for i in range(2)]
        shift = [sb(f"shift{i}", [P, 1]) for i in range(2)]
        top_v = sb("top_v", [P, SEGS * TOPK])
        top_e = sb("top_e", [P, SEGS * TOPK])
        top_s = sb("top_s", [P, SEGS])
        top_r = sb("top_r", [P, SEGS])
        logits = sb("logits", [P, PAIRS * E])
        r_val = sb("r_val", [P, PAIRS * 8])
        r_idx = sb("r_idx", [P, PAIRS * 8], U32)
        r_idxf = sb("r_idxf", [P, CHOICES * PAIRS])
        r_exp = sb("r_exp", [P, PAIRS])
        r_sum = sb("r_sum", [P, PAIRS])
        r_w = sb("r_w", [P, CHOICES * PAIRS])
        chosen = [xg_sb[:, k * PAIRS * E:(k + 1) * PAIRS * E] for k in range(CHOICES)]
        chosen_any = xg_sb[:, 2 * PAIRS * E:3 * PAIRS * E]
        route_tmp = xg_sb[:, 3 * PAIRS * E:4 * PAIRS * E]
        e_before = sb("e_before", [P, E])
        e_count = sb("e_count", [P, E])
        e_tiles = sb("e_tiles", [P, E])
        e_cum = sb("e_cum", [P, E])
        e_start = sb("e_start", [P, E])
        pos_f = sb("pos_f", [P, CHOICES * PAIRS])
        pos_i = sb("pos_i", [P, CHOICES * PAIRS], I32)
        hilo_i = sb("hilo_i", [P, CHOICES * PAIRS], I32)
        hi_f = sb("hi_f", [P, CHOICES * PAIRS])
        lo_f = sb("lo_f", [P, CHOICES * PAIRS])
        tile_e = sb("tile_e", [P, JW])
        tile_gu_at, tile_down_at = sb("tile_gu_at", [P, JW], I32), sb("tile_down_at", [P, JW], I32)
        lane_hot = [xg_sb[:, k * HOTS * P:(k + 1) * HOTS * P] for k in range(2)]
        tile_hot = [const_sb[:, k * HOTS * 2 * JW:(k + 1) * HOTS * 2 * JW] for k in range(2)]
        slot_token = sb("slot_token", [P, JW], I32)
        slot_w = sb("slot_w", [P, JW])
        gidx = [sb(f"gidx{i}", [P, 1], I32) for i in range(YBUFS)]

        bank = [stack.enter_context(nc.psum_tensor(f"bank{i}", [P, D], F32)) for i in range(8)]
        ps_x, ps_even, ps_odd, ps_corr, ps_T, ps_w_even, ps_w_odd, ps_out = bank
        ps_xgT, ps_gu, ps_y, ps_actT = bank[0], bank[6:8], bank[3:5], bank[5]
        ps_gate, ps_up, ps_shared = (bank[1], bank[7]), bank[2], (bank[0], bank[5], bank[3], bank[4])
        ps_slots, ps_rank, ps_total = bank[6], bank[3], bank[4]

        early_loaded, const_loaded = sem("early_loaded"), sem("const_loaded")
        x_loaded, ctx_loaded = [sem("x_loaded0"), sem("x_loaded1")], [sem("ctx_loaded0"), sem("ctx_loaded1")]
        gate_loaded, wgu_loaded, shgu_loaded = sem("gate_loaded"), sem("wgu_loaded"), sem("shgu_loaded")
        wd_loaded, shd_loaded = sem("wd_loaded"), sem("shd_loaded")
        x2_stored = [sem("x2_stored0"), sem("x2_stored1")]
        stats_done = [sem("x_stats_done"), sem("resid_stats_done")]
        meanvar_ready = [sem("x_meanvar_ready"), sem("resid_meanvar_ready")]
        veps_ready = [sem("x_veps_ready"), sem("resid_veps_ready")]
        root_ready = [sem("x_root_ready"), sem("resid_root_ready")]
        rstd_ready = [sem("x_rstd_ready"), sem("resid_rstd_ready")]
        matrices_hi_ready, matrices_lo_ready = sem("matrices_hi_ready"), sem("matrices_lo_ready")
        ctx_hi_ready, ctx_lo_ready = sem("ctx_hi_ready"), sem("ctx_lo_ready")
        xn_ready, x_spectrum = sem("xn_ready"), sem("x_spectrum")
        ctx_even_psum, ctx_even_ready = sem("ctx_even_psum"), sem("ctx_even_ready")
        ctx_odd_psum, ctx_odd_ready = sem("ctx_odd_psum"), sem("ctx_odd_ready")
        products_ready, corr_psum = sem("products_ready"), sem("corr_psum")
        maxima_ready, centered, lags_marked = sem("maxima_ready"), sem("centered"), sem("lags_marked")
        exp_ready, top_sum_ready, masked = sem("exp_ready"), sem("top_sum_ready"), sem("masked")
        top_r_ready = sem("top_r_ready")
        lagw_ready, lagwT_psum, lagwT_ready = sem("lagw_ready"), sem("lagwT_psum"), sem("lagwT_ready")
        w_even_psum, w_odd_psum = sem("w_even_psum"), sem("w_odd_psum")
        w_odd_sw_ready, odd_im_products = sem("w_odd_sw_ready"), sem("odd_im_products")
        odd_product_ready = sem("odd_product_ready")
        out_products_ready, out_psum, resid_ready = sem("out_products_ready"), sem("out_psum"), sem("resid_ready")
        x2n_ready, x2T_psum, x2T_ready, x2T_kept = sem("x2n_ready"), sem("x2T_psum"), sem("x2T_ready"), sem("x2T_kept")
        logits_psum, logits_ready = sem("logits_psum"), sem("logits_ready")
        route_step, route_diff, route_exp = sem("route_step"), sem("route_diff"), sem("route_exp")
        chosen_ready, counts_psum = sem("chosen_ready"), sem("counts_psum")
        lane_hot_ready, tile_hot_ready = sem("lane_hot_ready"), sem("tile_hot_ready")
        slots_psum, slots_ready = sem("slots_psum"), sem("slots_ready")
        tile_hot_found = sem("tile_hot_found")
        tile_e_ready, pos_ready = sem("tile_e_ready"), sem("pos_ready")
        sh_gate_psum, sh_up_psum, sh_silu = sem("sh_gate_psum"), sem("sh_up_psum"), sem("sh_silu")
        sh_act_ready, sh_out_psum, sh_added = sem("sh_act_ready"), sem("sh_out_psum"), sem("sh_added")
        tokens_hi_ready, tokens_lo_ready = sem("tokens_hi_ready"), sem("tokens_lo_ready")
        weights_hi_ready, weights_lo_ready = sem("weights_hi_ready"), sem("weights_lo_ready")
        act_hi_ready, act_lo_ready = sem("act_hi_ready"), sem("act_lo_ready")
        gidx_ready = sem("gidx_ready")
        gathered = [sem("gathered0"), sem("gathered1")]
        xgT_psum, xgT_ready, gu_psum, silu_ready = sem("xgT_psum"), sem("xgT_ready"), sem("gu_psum"), sem("silu_ready")
        act_ready, actT_psum, actT_ready = sem("act_ready"), sem("actT_psum"), sem("actT_ready")
        down_psum, y_ready = sem("down_psum"), sem("y_ready")
        y_stored = [sem("y_stored0"), sem("y_stored1")]
        y_gathered = [sem(f"y_gathered{i}") for i in range(YBUFS)]
        yidx_ready, y_half_added, y_added = sem("yidx_ready"), sem("y_half_added"), sem("y_added")
        out_stored = sem("out_stored")
        dve_passed, pool_passed = sem("dve_passed"), sem("pool_passed")

        def tile_of(tensor, p):
            return tensor[:, bass.ds(p * D, D)]

        def by_tile(ap):
            return ap.rearrange("p (t n) -> p t n", t=GT)

        def by_choice(ap, n):
            return ap.rearrange("p (i l) -> p i l", i=n)

        def weight_block(w, part, m):
            return w[:, :].rearrange("p (c o) -> p c o", c=KB)[:, :, part * SHARED + m * P:part * SHARED + (m + 1) * P]

        WEIGHT_BLOCKS = [(i % 2, i // 2) for i in range(1, 2 * SB)] + [(0, 0)]

        def segs(ap):
            return ap.rearrange("p (s l) -> p s l", s=SEGS)

        def schedule(iteration):
            for i in range(-2, 4):
                iteration(i // 2, i % 2, i)
            return range(2, (PAIRS - 2) // 2), [(i // 2, i % 2, i) for i in range(PAIRS - 2, PAIRS + 3)]

        def live(n, d):
            return n is None or 0 <= n + d < PAIRS

        def pair(h, b, d):
            return 2 * h + (b + d), (b + d) % 2

        def half(h, b, d):
            return h + (b + d) // 2

        def run(eng, iteration):
            hs, last = schedule(iteration)
            with eng.Fori(hs.start, hs.stop) as h:
                for b in range(2):
                    iteration(h, b, None)
            for h, b, n in last:
                iteration(h, b, n)

        block = stack.enter_context(nc.Block())

        @block.sync
        def _(sp):
            def load_pair(h, b):
                p = 2 * h + b
                wait(sp, ctx_odd_psum, p - 1)
                wait(sp, stats_done[0], p - 1)
                sp.dma_start(tile_of(resid, p), x[bass.ds(p * P, P), :]).then_inc(x_loaded[b], 16)
                sp.dma_start(ctx_in[b], ctx[bass.ds(p * P, P), :]).then_inc(ctx_loaded[b], 16)

            def load_expert_pair(h):
                width = 2 * KB * 2 * INTER
                sp.dma_start(wgu_sb[:, bass.ds(h * width, width)],
                             w_gu[:, bass.ds(h * width, width)]).then_inc(wgu_loaded, 16)

            def iteration(h, b, n):
                if live(n, 2) and n != -2:
                    load_pair(h + 1, b)
                if live(n, -2):
                    p, pb = pair(h, b, -2)
                    sp.wait_ge(x2n_ready, p + 1)
                    sp.dma_start(x2_rows[bass.ds(p * P, P), :], x2n[pb]).then_inc(x2_stored[pb], 16)
                if n == 2:
                    sp.dma_start(shgu_sb[:, :], sh_gu[:, :]).then_inc(shgu_loaded, 16)
                if b == 1 and (n is None or 1 <= n < PAIRS):
                    wait(sp, wgu_loaded, 16 * h)
                    if n == PAIRS - 1:
                        sp.wait_ge(ctx_odd_psum, PAIRS)
                    load_expert_pair(h)

            sp.dma_start(tile_of(resid, 0), x[0:P, :]).then_inc(x_loaded[0], 16)
            sp.dma_start(const_sb[:, 0:EARLY], consts[:, 0:EARLY]).then_inc(early_loaded, 16)
            sp.dma_start(ctx_in[0], ctx[0:P, :]).then_inc(ctx_loaded[0], 16)
            sp.dma_start(const_sb[:, EARLY:], consts[:, EARLY:]).then_inc(const_loaded, 16)
            sp.dma_start(gate_sb[:, :], gate[:, :]).then_inc(gate_loaded, 16)
            run(sp, iteration)
            sp.wait_ge(logits_psum, PAIRS)
            sp.wait_ge(x2T_kept, PAIRS)
            for b in range(2):
                sp.wait_ge(x2_stored[b], 16 * PAIRS // 2)
            sp.dma_start(shd_sb, sh_down[:, :]).then_inc(shd_loaded, 16)
            sp.dma_start(wd_sb[:, 0:EARLY_DOWN], w_down[:, 0:EARLY_DOWN]).then_inc(wd_loaded, 16)
            for t in range(GT):
                sp.wait_ge(sh_out_psum, t + 1)
                cols = slice(EARLY_DOWN + t * D, EARLY_DOWN + (t + 1) * D)
                sp.dma_start(wd_sb[:, cols], w_down[:, cols]).then_inc(wd_loaded, 16)

            def store_y(h, b):
                j = 2 * h + b
                sp.wait_ge(y_ready, j + 1)
                sp.dma_start(y_rows[bass.ds(j * P, P), :], y_out[b]).then_inc(y_stored[b], 16)

            with sp.Fori(0, SLOT_TILES // 2) as h:
                for b in range(2):
                    store_y(h, b)
            store_y(SLOT_TILES // 2, 0)
            with sp.Fori(0, PAIRS) as t:
                sp.wait_ge(y_added, t + 1)
                sp.wait_ge(sh_added, t + 1)
                sp.dma_start(out[bass.ds(t * P, P), :], tile_of(resid, t)).then_inc(out_stored, 16)
            sp.wait_ge(out_stored, 16 * PAIRS)

        @block.tensor
        def _(pe):
            mm = nc.tensor.matmul

            def split_product(ps, a, b, start, stop):
                terms = ((0, 0), (0, 1), (1, 0))
                for n, (i, k) in enumerate(terms):
                    last = mm(ps, a[i], b[k], start=start and n == 0, stop=stop and n == len(terms) - 1)
                return last

            def of_halves(halves, pick):
                return tuple(pick(half) for half in halves)

            def output(p):
                wait(pe, resid_ready, p)
                pe.wait_ge(out_products_ready, 2 * p + 1)
                mm(ps_out[:, :], C["out_even_plain"], out_prod[0], start=True, stop=False)
                mm(ps_out[:, :], C["out_even_swapped"], out_prod[1], start=False, stop=False)
                pe.wait_ge(odd_product_ready, p + 1)
                mm(ps_out[:, :], C["out_odd"], odd_prod, start=False, stop=True).then_inc(out_psum, 1)

            def iteration(h, b, n):
                if n == 0:
                    pe.wait_ge(const_loaded, 16)
                    pe.wait_ge(gate_loaded, 16)
                if live(n, 0):
                    p, _ = pair(h, b, 0)
                    pe.wait_ge(products_ready, p + 1)
                    wait(pe, lags_marked, p)
                    for c in range(KB):
                        cols = slice(c * P, (c + 1) * P)
                        mm(ps_corr[:, cols], prod_plain[:, cols], C["corr_plain"], start=True, stop=False)
                        last = mm(ps_corr[:, cols], prod_swapped[:, cols], C["corr_swapped"], start=False, stop=True)
                    last.then_inc(corr_psum, 1)
                if n == PAIRS:
                    shared_half(0, 0, 0, range(2, KB))
                if live(n, -1):
                    p, _ = pair(h, b, -1)
                    pe.wait_ge(lagw_ready, p + 1)
                    wait(pe, x2T_ready, p - 1)
                    for c in range(KB):
                        cols = slice(c * P, (c + 1) * P)
                        last = nc.tensor.transpose(ps_T[:, cols], lagw[:, cols], C["identity"])
                    last.then_inc(lagwT_psum, 1)
                if n == PAIRS:
                    output(PAIRS - 2)
                if n == PAIRS + 2:
                    shared_half(0, 1, 0, range(2, 3))
                if live(n, -3):
                    p, pb = pair(h, b, -3)
                    pe.wait_ge(x2T_ready, p + 1)
                    for c in range(KB):
                        last = mm(ps_w_even[:, 0:E], x2T_tile[pb][:, c * P:(c + 1) * P], gate_sb[:, c * E:(c + 1) * E],
                                  start=c == 0, stop=c == KB - 1)
                    last.then_inc(logits_psum, 1)
                if n == PAIRS + 1:
                    shared_half(0, 0, 1, range(2, KB))
                    pe.wait_ge(resid_ready, PAIRS)
                    shared_half(0, 1, 0, range(2))
                if live(n, -1):
                    p, _ = pair(h, b, -1)
                    pe.wait_ge(lagwT_ready, p + 1)
                    mm(ps_w_odd[:, :], C["odd"], lagwT, start=True, stop=True).then_inc(w_odd_psum, 1)
                    wait(pe, logits_ready, p - 1)
                    mm(ps_w_even[:, :], C["even"], lagwT, start=True, stop=True).then_inc(w_even_psum, 1)
                if live(n, 1):
                    p, pb = pair(h, b, 1)
                    pe.wait_ge(ctx_lo_ready, p + 1)
                    wait(pe, ctx_even_ready, p)
                    split_product(ps_even[:, :], of_halves(matrices_halves, lambda w: w[:, 0:P]), ctx_halves,
                                  True, True).then_inc(ctx_even_psum, 1)
                    pe.wait_ge(xn_ready, p + 1)
                    wait(pe, products_ready, p)
                    mm(ps_x[:, :], C["even"], xn, start=True, stop=True).then_inc(x_spectrum, 1)
                    wait(pe, ctx_odd_ready, p)
                    split_product(ps_odd[:, :], of_halves(matrices_halves, lambda w: w[:, P:2 * P]), ctx_halves,
                                  True, True).then_inc(ctx_odd_psum, 1)
                if n == PAIRS - 1:
                    pe.wait_ge(shgu_loaded, 16)
                    pe.wait_ge(x2T_kept, GT)
                    pe.wait_ge(ctx_even_ready, PAIRS)
                    pe.wait_ge(ctx_odd_ready, PAIRS)
                    shared_half(0, 0, 0, range(2))
                if n == PAIRS:
                    shared_half(0, 0, 1, range(2))
                if live(n, -2):
                    p, pb = pair(h, b, -2)
                    pe.wait_ge(x2n_ready, p + 1)
                    for c in range(KB):
                        cols = slice(c * P, (c + 1) * P)
                        last = nc.tensor.transpose(ps_T[:, cols], x2n[pb][:, cols], C["identity"])
                    last.then_inc(x2T_psum, 1)
                if live(n, -1) and n != PAIRS - 1:
                    output(pair(h, b, -1)[0])

            def shared_tokens(g, c):
                cols = x2T[:, bass.ds(g * GT * D, GT * D)]
                return cols.rearrange("p (t c n) -> p c t n", t=GT, c=KB)[:, c]

            def shared_half(g, m, part, blocks=range(KB)):
                ps, done, read = ((ps_gate[m % 2], sh_gate_psum, sh_silu), (ps_up, sh_up_psum, sh_act_ready))[part]
                if 0 in blocks:
                    wait(pe, read, g * SB + m + part - 1)
                for c in blocks:
                    col = c * 2 * SHARED + part * SHARED + m * P
                    last = mm(ps[:, :].rearrange("p (t n) -> p t n", t=GT), shgu_sb[:, col:col + P], shared_tokens(g, c),
                              start=c == 0, stop=c == KB - 1)
                if KB - 1 in blocks:
                    last.then_inc(done, 1)

            def shared_down(g, t):
                if t == 0:
                    pe.wait_ge(sh_act_ready, (g + 1) * SB)
                for m in range(SB):
                    last = mm(ps_shared[t][:, :], sh_act[:, (t * SB + m) * P:(t * SB + m + 1) * P],
                              shd_sb[:, m * D:(m + 1) * D], start=m == 0, stop=m == SB - 1)
                last.then_inc(sh_out_psum, 1)

            def split_half(g, m, part):
                ps, done, read = ((ps_gate[m % 2], sh_gate_psum, sh_silu), (ps_up, sh_up_psum, sh_act_ready))[part]
                pe.wait_ge(read, g * SB + m + part - 1)
                if m == 0 and part == 0:
                    pe.wait_ge(tokens_lo_ready, g * GT)
                first = part * SHARED + m * P
                for c in range(KB):
                    col = c * 2 * SHARED + first
                    last = split_product(ps[:, :].rearrange("p (t n) -> p t n", t=GT),
                                         of_halves(shgu_halves, lambda w: w[:, col:col + P]),
                                         of_halves(tokens_halves, lambda x: x[:, :].rearrange("p (t c n) -> p c t n", t=GT, c=KB)[:, c]),
                                         c == 0, c == KB - 1)
                last.then_inc(done, 1)

            def split_down(g):
                first = [(t, m) for t in range(2) for m in range(SB - 1)] + [(t, SB - 1) for t in range(2)]
                for t, m in first + [(t, m) for t in range(2, GT) for m in range(SB)]:
                    if m == 0:
                        pe.wait_ge(sh_added, (g - 1) * GT + t + 1)
                    if t == 0:
                        pe.wait_ge(act_lo_ready, (g - 1) * SB + m + 1)
                    last = split_product(ps_shared[t][:, :],
                                         of_halves(act_halves, lambda a: a[:, m * D + t * P:m * D + (t + 1) * P]),
                                         of_halves(shd_halves, lambda w: w[:, m * D:(m + 1) * D]), m == 0, m == SB - 1)
                    if m == SB - 1:
                        last.then_inc(sh_out_psum, 1)

            pe.wait_ge(matrices_lo_ready, 1)

            run(pe, iteration)

            shared_half(0, 1, 0, range(3, KB))
            pe.wait_ge(logits_ready, PAIRS)
            shared_half(0, 1, 1)
            pe.wait_ge(chosen_ready, 1)
            mm(ps_rank[:, 0:PAIRS * E], C["earlier"], chosen_any, start=True, stop=True)
            mm(ps_total[:, 0:PAIRS * E], C["ones"], chosen_any, start=True, stop=True).then_inc(counts_psum, 1)

            def slots(turns):
                for s in turns:
                    pe.wait_ge(lane_hot_ready, s + 1)
                    pe.wait_ge(tile_hot_ready, s + 1)
                    for i in range(HOTS):
                        last = mm(ps_slots[:, 0:2 * JW], lane_hot[s % 2][:, i * P:(i + 1) * P],
                                  tile_hot[s % 2].rearrange("p (v i j) -> p v i j", v=2, i=HOTS)[:, :, i],
                                  start=s == 0 and i == 0, stop=True, skip_group_check=True)
                    last.then_inc(slots_psum, 1)

            shared_half(0, 2, 0)
            shared_half(0, 2, 1)
            shared_half(0, 3, 0)
            shared_half(0, 3, 1)
            slots(range(0, 2))
            pe.wait_ge(shd_loaded, 16)
            shared_down(0, 0)
            slots(range(2, 4))
            shared_down(0, 1)
            slots(range(4, HOT_TURNS))

            def transposes(h, b):
                j = 2 * h + b
                pe.wait_ge(gathered[b], 16 * (h + 1))
                wait(pe, xgT_ready, j)
                for c in range(KB):
                    cols = slice(c * P, (c + 1) * P)
                    last = nc.tensor.transpose(ps_xgT[:, cols], xg[b][:, cols], C["identity"])
                last.then_inc(xgT_psum, 1)

            def weights_at(starts, j, width):
                return pe.value_load(starts[0:1, bass.ds(j, 1)], min_val=0, max_val=(E - 1) * width)

            def expert(h, b, n):
                j = 2 * h + b
                if n is None or n < SLOT_TILES:
                    at = weights_at(tile_gu_at, j, KB * 2 * INTER)
                    pe.wait_ge(xgT_ready, j + 1)
                    for c in range(KB):
                        last = mm(ps_gu[b][:, 0:2 * INTER], xgT[b][:, c * P:(c + 1) * P],
                                  wgu_sb[:, bass.ds(at + c * 2 * INTER, 2 * INTER)],
                                  start=c == 0, stop=c == KB - 1)
                    last.then_inc(gu_psum, 1)
                if n is None or 1 <= n < SLOT_TILES - 1:
                    transposes(h + (b + 1) // 2, (b + 1) % 2)
                if n is None or 1 <= n <= SLOT_TILES:
                    pe.wait_ge(act_ready, j)
                    wait(pe, actT_ready, j - 1)
                    nc.tensor.transpose(ps_actT[:, 0:P], act_sb[:, :], C["identity"]).then_inc(actT_psum, 1)
                if n is None or n >= 2:
                    at = weights_at(tile_down_at, j - 2, D)
                    if n == SLOT_TILES + 1:
                        pe.wait_ge(actT_ready, j - 1)
                    wait(pe, y_ready, j - 3 if n is None or n > 2 else 0)
                    mm(ps_y[b][:, :], actT_sb[b], wd_sb[:, bass.ds(at, D)], start=True, stop=True).then_inc(down_psum, 1)

            shared_down(0, 2)
            pe.wait_ge(tile_e_ready, 1)
            pe.wait_ge(sh_added, 1)
            transposes(0, 0)
            shared_down(0, 3)
            transposes(0, 1)
            pe.wait_ge(wgu_loaded, 16 * E // 2)
            pe.wait_ge(slots_ready, 1)
            for n in range(4):
                if n == 1:
                    pe.wait_ge(sh_added, GT)
                if n == 2:
                    pe.wait_ge(wd_loaded, 16 * (1 + GT))
                expert(n // 2, n % 2, n)
            with pe.Fori(2, SLOT_TILES // 2) as h:
                for b in range(2):
                    expert(h, b, None)
            expert(SLOT_TILES // 2, 0, SLOT_TILES - 1)
            shared_half(1, 0, 0)
            for n in range(SLOT_TILES, SLOT_TILES + 2):
                expert(n // 2, n % 2, n)
            pe.wait_ge(tokens_lo_ready, GT)
            for i, (part, m) in enumerate(WEIGHT_BLOCKS[:-1]):
                pe.wait_ge(weights_lo_ready, i + 1)
                split_half(1, m, part)
            pe.wait_ge(weights_lo_ready, len(WEIGHT_BLOCKS) + SB)
            pe.wait_ge(xgT_ready, SLOT_TILES)
            pe.wait_ge(actT_ready, SLOT_TILES)
            pe.wait_ge(y_ready, SLOT_TILES)
            split_down(1)
            with pe.Fori(2, GROUPS) as g:
                for m in range(SB):
                    for part in range(2):
                        split_half(g, m, part)
                split_down(g)

        @block.scalar
        def _(act):
            copy = nc.scalar.copy

            def shared_silu(g, m):
                n = g * SB + m
                act.wait_ge(sh_gate_psum, n + 1)
                wait(act, sh_act_ready, n)
                nc.scalar.activation(silu_sb[:, :], ps_gate[m % 2][:, :], ACT.Silu).then_inc(sh_silu, 1)

            def normalise(which, dst, src, p, done):
                act.wait_ge(rstd_ready[which], p + 1)
                nc.scalar.activation(dst, src, ACT.Identity, bias=shift[which][:, :], scale=rstd[which][:, :]).then_inc(done, 1)

            def even_context(h, b, n):
                if live(n, 1):
                    p, pb = pair(h, b, 1)
                    act.wait_ge(ctx_even_psum, p + 1)
                    wait(act, out_products_ready, 2 * (p - 1) - 1)
                    copy(ctx_even[pb], ps_even[:, :])
                    copy(ctx_even_sw[pb][0:64, :], ps_even[64:128, :])
                    copy(ctx_even_sw[pb][64:128, :], ps_even[0:64, :]).then_inc(ctx_even_ready, 1)

            def ahead(h, b, n):
                if live(n, 2):
                    p, pb = pair(h, b, 2)
                    act.wait_ge(ctx_loaded[pb], 16 * (half(h, b, 2) + 1))
                    wait(act, ctx_odd_psum, p)
                    copy(ctx_halves[0], ctx_in[pb]).then_inc(ctx_hi_ready, 1)
                if live(n, 2):
                    p, _ = pair(h, b, 2)
                    wait(act, x_spectrum, p)
                    normalise(0, xn, tile_of(resid, p), p, xn_ready)

            def iteration(h, b, n):
                if live(n, -1):
                    p, _ = pair(h, b, -1)
                    act.wait_ge(lagwT_psum, p + 1)
                    wait(act, w_even_psum, p)
                    copy(lagwT, ps_T[:, :]).then_inc(lagwT_ready, 1)
                if n == PAIRS + 2:
                    act.wait_ge(x2T_ready, PAIRS)
                    copy(tile_of(x2T, PAIRS - 1), x2T_tile[(PAIRS - 1) % 2]).then_inc(x2T_kept, 1)
                if live(n, -3):
                    p, _ = pair(h, b, -3)
                    act.wait_ge(logits_psum, p + 1)
                    copy(logits[:, bass.ds(p * E, E)], ps_w_even[:, 0:E]).then_inc(logits_ready, 1)
                if n == PAIRS + 1:
                    shared_silu(0, 0)
                if n == 0:
                    even_context(h, b, n)
                if live(n, 0):
                    p, _ = pair(h, b, 0)
                    act.wait_ge(centered, p + 1)
                    nc.scalar.activation(top_e[:, :], top_e[:, :], ACT.Exp)
                    nc.scalar.activation(expz, expz, ACT.Exp).then_inc(exp_ready, 1)
                if live(n, -1):
                    p, _ = pair(h, b, -1)
                    act.wait_ge(w_odd_psum, p + 1)
                    wait(act, odd_product_ready, p)
                    copy(w_odd_sw[0:64, :], ps_w_odd[64:128, :])
                    nc.scalar.mul(w_odd_sw[64:128, :], ps_w_odd[0:64, :], -1.0).then_inc(w_odd_sw_ready, 1)
                if live(n, -2):
                    p, pb = pair(h, b, -2)
                    wait(act, x2T_psum, p - 1)
                    wait(act, x2_stored[pb], 16 * half(h, b, -2))
                    normalise(1, x2n[pb], tile_of(resid, p), p, x2n_ready)
                if n != 0:
                    even_context(h, b, n)
                if live(n, -2):
                    p, pb = pair(h, b, -2)
                    act.wait_ge(x2T_psum, p + 1)
                    wait(act, x2T_kept, p - 1)
                    wait(act, logits_psum, p - 1)
                    copy(x2T_tile[pb], ps_T[:, :]).then_inc(x2T_ready, 1)
                if n == -1:
                    ahead(h, b, n)
                if live(n, 1):
                    p, pb = pair(h, b, 1)
                    act.wait_ge(ctx_odd_psum, p + 1)
                    wait(act, odd_product_ready, p - 1)
                    copy(ctx_odd_re[pb][0:64, :], ps_odd[0:64, :])
                    copy(ctx_odd_re[pb][64:128, :], ps_odd[0:64, :])
                    copy(ctx_odd_im[pb][0:64, :], ps_odd[64:128, :])
                    copy(ctx_odd_im[pb][64:128, :], ps_odd[64:128, :]).then_inc(ctx_odd_ready, 1)
                if n != -1:
                    ahead(h, b, n)

            act.wait_ge(early_loaded, 16)
            copy(matrices_halves[0], C["context"]).then_inc(matrices_hi_ready, 1)
            run(act, iteration)

            act.wait_ge(route_diff, 1)
            nc.scalar.activation(r_exp[:, :], r_exp[:, :], ACT.Exp).then_inc(route_exp, 1)

            for m in range(1, SB):
                shared_silu(0, m)

            def gathered_T(h, b):
                j = 2 * h + b
                act.wait_ge(xgT_psum, j + 1)
                wait(act, gu_psum, j - 1)
                copy(xgT[b], ps_xgT[:, :]).then_inc(xgT_ready, 1)

            def expert(h, b, n):
                j = 2 * h + b
                if n is None or n + 1 < SLOT_TILES:
                    gathered_T(h + (b + 1) // 2, (b + 1) % 2)
                act.wait_ge(gu_psum, j + 1)
                wait(act, act_ready, j)
                nc.scalar.activation(silu_sb[:, 0:INTER], ps_gu[b][:, 0:INTER], ACT.Silu).then_inc(silu_ready, 1)

            act.wait_ge(sh_up_psum, SB)
            gathered_T(0, 0)
            for n in range(2):
                expert(0, n, n)
            with act.Fori(1, SLOT_TILES // 2) as h:
                for b in range(2):
                    expert(h, b, None)
            expert(SLOT_TILES // 2, 0, SLOT_TILES - 1)

            def weights_hi(first, last):
                for part, m in WEIGHT_BLOCKS[first:last]:
                    copy(weight_block(shgu_hi, part, m), weight_block(shgu_sb, part, m)).then_inc(weights_hi_ready, 1)

            def down_weights_hi(m):
                copy(shd_hi[:, m * D:(m + 1) * D], shd_sb[:, m * D:(m + 1) * D]).then_inc(weights_hi_ready, 1)

            def split_tokens_hi(g):
                for t in range(GT):
                    act.wait_ge(sh_up_psum, g * SB)
                    copy(tokens_halves[0][:, t * D:(t + 1) * D], tile_of(x2T, g * GT + t)).then_inc(tokens_hi_ready, 1)

            def split_act_hi(g, m):
                wait(act, sh_out_psum, g * GT)
                act.wait_ge(sh_act_ready, g * SB + m + 1)
                copy(by_tile(act_halves[0][:, m * D:(m + 1) * D]), act_block(m)).then_inc(act_hi_ready, 1)

            act.wait_ge(gu_psum, SLOT_TILES)
            split_tokens_hi(1)
            weights_hi(0, 3)
            act.wait_ge(act_ready, SLOT_TILES)
            for m in range(SB):
                shared_silu(1, m)
                weights_hi(3 + 2 * m, 5 + 2 * m)
                split_act_hi(1, m)
                if m == 1:
                    act.wait_ge(down_psum, SLOT_TILES)
                if 1 <= m <= 2:
                    down_weights_hi(2 * m - 2)
                    down_weights_hi(2 * m - 1)
            split_tokens_hi(2)
            for g in range(2, GROUPS - 1):
                for m in range(SB):
                    shared_silu(g, m)
                    split_act_hi(g, m)
                split_tokens_hi(g + 1)
            for m in range(SB):
                shared_silu(GROUPS - 1, m)
                split_act_hi(GROUPS - 1, m)

        @block.vector
        def _(dve):
            tt, ts, stt = nc.vector.tensor_tensor, nc.vector.tensor_scalar, nc.vector.scalar_tensor_tensor

            def shared_multiply(g, m):
                dve.wait_ge(sh_silu, g * SB + m + 1)
                dve.wait_ge(sh_up_psum, g * SB + m + 1)
                tt(act_block(m), by_tile(ps_up[:, :]), by_tile(silu_sb[:, :]), ALU.mult).then_inc(sh_act_ready, 1)

            def moments(which, src, p):
                nc.vector.bn_stats(stats[which][:, :], src).then_inc(stats_done[which], 1)
                dve.wait_ge(stats_done[which], p + 1)
                apart(dve, dve_passed)
                nc.vector.bn_aggr(meanvar[which][:, :], stats[which][:, :]).then_inc(meanvar_ready[which], 1)

            def products(h, b, n):
                if live(n, 1):
                    p, pb = pair(h, b, 1)
                    dve.wait_ge(x_spectrum, p + 1)
                    dve.wait_ge(ctx_even_ready, p + 1)
                    tt(prod_plain, ps_x[:, :], ctx_even[pb], ALU.mult)
                    tt(prod_swapped, ps_x[:, :], ctx_even_sw[pb], ALU.mult).then_inc(products_ready, 1)

            def moments_ahead(h, b, n):
                if live(n, 2):
                    p, pb = pair(h, b, 2)
                    wait(dve, xn_ready, p)
                    dve.wait_ge(x_loaded[pb], 16 * (half(h, b, 2) + 1))
                    apart(dve, dve_passed)
                    moments(0, tile_of(resid, p), p)

            def iteration(h, b, n):
                if live(n, -2):
                    p, pb = pair(h, b, -2)
                    dve.wait_ge(out_psum, p + 1)
                    tt(tile_of(resid, p), ps_out[:, :], tile_of(resid, p), ALU.add).then_inc(resid_ready, 1)
                    dve.wait_ge(resid_ready, p + 1)
                    apart(dve, dve_passed)
                    moments(1, tile_of(resid, p), p)
                if n == PAIRS + 1:
                    shared_multiply(0, 0)
                if live(n, 0):
                    p, _ = pair(h, b, 0)
                    dve.wait_ge(corr_psum, p + 1)
                    apart(dve, dve_passed)
                    lags, tops = segs(ps_corr[:, :]), segs(top_v[:, :])
                    for s in range(SEGS):
                        last = nc.vector.max(tops[:, s], lags[:, s])
                    last.then_inc(maxima_ready, 1)
                    dve.wait_ge(maxima_ready, p + 1)
                    largest = tops[:, :, 0:1]
                    tt(segs(top_e[:, :]), tops, largest.to_broadcast([P, SEGS, TOPK]), ALU.subtract)
                    tt(segs(expz), lags, largest.to_broadcast([P, SEGS, L]), ALU.subtract).then_inc(centered, 1)
                    wait(dve, lagwT_psum, p)
                    apart(dve, dve_passed)
                    for s in range(SEGS):
                        last = nc.vector.match_replace(segs(lagw)[:, s], tops[:, s], lags[:, s], TAKEN)
                    last.then_inc(lags_marked, 1)
                if live(n, -1):
                    p, pb = pair(h, b, -1)
                    dve.wait_ge(w_even_psum, p + 1)
                    tt(out_prod[0], ps_w_even[:, :], ctx_even[pb], ALU.mult)
                    tt(out_prod[1], ps_w_even[:, :], ctx_even_sw[pb], ALU.mult).then_inc(out_products_ready, 1)
                if n == 0:
                    products(h, b, n)
                if live(n, 0):
                    p, _ = pair(h, b, 0)
                    dve.wait_ge(exp_ready, p + 1)
                    nc.vector.reduce_sum(top_s[:, :], segs(top_e[:, :]), axis=AX.X).then_inc(top_sum_ready, 1)
                    dve.wait_ge(lags_marked, p + 1)
                    stt(lagw, lagw, TAKEN, expz, ALU.is_equal, ALU.mult).then_inc(masked, 1)
                    dve.wait_ge(top_sum_ready, p + 1)
                    nc.vector.reciprocal(top_r[:, :], top_s[:, :]).then_inc(top_r_ready, 1)
                if live(n, -1):
                    p, pb = pair(h, b, -1)
                    dve.wait_ge(w_odd_sw_ready, p + 1)
                    dve.wait_ge(ctx_odd_ready, p + 1)
                    tt(odd_prod, ps_w_odd[:, :], ctx_odd_re[pb], ALU.mult).then_inc(out_products_ready, 1)
                if n == -1:
                    moments_ahead(h, b, n)
                if n != 0:
                    products(h, b, n)
                if n != -1:
                    moments_ahead(h, b, n)
                if n == -2:
                    dve.wait_ge(matrices_hi_ready, 1)
                    tt(matrices_halves[1], C["context"], matrices_halves[0].bitcast(F32), ALU.subtract).then_inc(matrices_lo_ready, 1)
                    dve.wait_ge(ctx_hi_ready, 1)
                    tt(ctx_halves[1], ctx_in[0], ctx_halves[0].bitcast(F32), ALU.subtract).then_inc(ctx_lo_ready, 1)

            run(dve, iteration)
            dve.wait_ge(const_loaded, 16)

            steps = [0]

            def then(ins):
                steps[0] += 1
                ins.then_inc(route_step, 1)
                dve.wait_ge(route_step, steps[0])

            def by_expert(ap):
                return ap.rearrange("p (t e) -> p t e", e=E)

            def expert_major(ap):
                return ap.rearrange("p (e t) -> p e t", e=E)

            def over(ap, dims, axis):
                return ap.unsqueeze(axis).to_broadcast(dims)

            dve.wait_ge(logits_ready, PAIRS)
            dve.wait_ge(x2T_kept, PAIRS)
            vals, idx = r_val[:, :].rearrange("p (t v) -> p t v", v=8), r_idx[:, :].rearrange("p (t v) -> p t v", v=8)
            log_t = by_expert(logits[:, :])
            for t in range(PAIRS):
                last = nc.vector.max(vals[:, t], log_t[:, t])
            then(last)
            for t in range(PAIRS):
                last = nc.vector.max_index(idx[:, t], vals[:, t], log_t[:, t])
            tt(r_exp[:, :], vals[:, :, 1], vals[:, :, 0], ALU.subtract).then_inc(route_diff, 1)
            then(last)
            idxf = r_idxf[:, :].rearrange("p (k t) -> p k t", k=CHOICES)
            then(nc.vector.tensor_copy(idxf, idx[:, :, 0:CHOICES].rearrange("p t k -> p k t")))
            dims = [P, PAIRS, E]
            for k in range(CHOICES):
                last = tt(by_expert(chosen[k]), over(C["count"][:, 0:E], dims, 1), over(idxf[:, k], dims, 2), ALU.is_equal)
            then(last)
            tt(chosen_any, chosen[0], chosen[1], ALU.add).then_inc(chosen_ready, 1)

            def shared_add(g, t):
                dve.wait_ge(sh_out_psum, g * GT + t + 1)
                dst = tile_of(resid, g * GT + t)
                tt(dst, ps_shared[t][:, :], dst, ALU.add).then_inc(sh_added, 1)

            dve.wait_ge(shd_loaded, 16)
            wts = r_w[:, :].rearrange("p (k t) -> p k t", k=CHOICES)
            dve.wait_ge(route_exp, 1)
            then(ts(r_sum[:, :], r_exp[:, :], 1.0, None, ALU.add))
            then(nc.vector.reciprocal(wts[:, 0], r_sum[:, :]))
            then(tt(wts[:, 1], r_exp[:, :], wts[:, 0], ALU.mult))
            dve.wait_ge(counts_psum, 1)
            totals3, cumul3 = expert_major(totals), expert_major(cumul)
            then(nc.vector.tensor_copy(totals3, by_expert(ps_total[:, 0:PAIRS * E]).rearrange("p t e -> p e t")))
            then(nc.vector.tensor_tensor_scan(cumul, C["ones"][:, 0:1].to_broadcast([P, E * PAIRS]), totals, 0.0, ALU.mult, ALU.add))
            nc.vector.memset(e_before[:, 0:1], 0.0)
            then(nc.vector.tensor_copy(e_before[:, 1:E], cumul3[:, 0:E - 1, PAIRS - 1]))
            then(tt(e_count[:, :], cumul3[:, :, PAIRS - 1], e_before[:, :], ALU.subtract))
            edges = expert_major(route_tmp)
            then(tt(edges, over(e_count[:, :], [P, E, E], 2), over(C["tile_edge"], [P, E, E], 1), ALU.is_gt))
            then(nc.vector.reduce_sum(e_tiles[:, :], edges, axis=AX.X))
            then(nc.vector.tensor_tensor_scan(e_cum[:, :], C["ones"][:, 0:E], e_tiles[:, :], 0.0, ALU.mult, ALU.add))
            then(tt(e_start[:, :], e_cum[:, :], e_tiles[:, :], ALU.subtract))
            shared_multiply(0, 1)
            then(stt(e_start[:, :], e_start[:, :], float(P), e_before[:, :], ALU.mult, ALU.subtract))
            then(tt(cumul, cumul, totals, ALU.subtract))
            then(tt(cumul3, cumul3, over(e_start[:, :], [P, E, PAIRS], 2), ALU.add))
            then(tt(by_expert(totals), by_expert(ps_rank[:, 0:PAIRS * E]), cumul3.rearrange("p e t -> p t e"), ALU.add))
            pos = pos_f[:, :].rearrange("p (k t) -> p k t", k=CHOICES)
            for k in range(CHOICES):
                then(tt(route_tmp, chosen[k], totals, ALU.mult))
                then(nc.vector.reduce_sum(pos[:, k], by_expert(route_tmp), axis=AX.X))
            nc.vector.tensor_copy(pos_i[:, :], pos_f[:, :]).then_inc(pos_ready, 1)
            dve.wait_ge(pos_ready, 1)
            then(nc.vector.tensor_scalar(hilo_i[:, :], pos_i[:, :], 7, None, ALU.logical_shift_right))
            then(nc.vector.tensor_copy(hi_f[:, :], hilo_i[:, :]))
            then(nc.vector.tensor_scalar(hilo_i[:, :], pos_i[:, :], P - 1, None, ALU.bitwise_and))
            then(nc.vector.tensor_copy(lo_f[:, :], hilo_i[:, :]))
            shared_multiply(0, 2)
            step = PAIRS
            for j in range(0, JW, step):
                ended = route_tmp.rearrange("p (j e) -> p j e", e=E)
                then(tt(ended, over(e_cum[:, :], [P, step, E], 1), over(C["count"][:, j:j + step], [P, step, E], 2), ALU.is_le))
                then(nc.vector.reduce_sum(tile_e[:, j:j + step], ended, axis=AX.X))
            then(nc.vector.tensor_scalar(tile_e[:, :], tile_e[:, :], float(E - 1), float(D), ALU.min, ALU.mult))
            nc.vector.tensor_copy(tile_down_at[:, :], tile_e[:, :])
            nc.vector.tensor_scalar(tile_gu_at[:, :], tile_e[:, :], float(KB * 2 * INTER // D), None, ALU.mult).then_inc(tile_e_ready, 1)

            for s in range(HOT_TURNS):
                wait(dve, slots_psum, s - 1)
                turn = slice(s * HOTS, (s + 1) * HOTS)
                tt(by_choice(tile_hot[s % 2], 2 * HOTS)[:, 0:HOTS], over(C["count"][:, 0:JW], [P, HOTS, JW], 1),
                   over(hi_f[:, turn], [P, HOTS, JW], 2), ALU.is_equal).then_inc(tile_hot_found, 1)
                tt(by_choice(lane_hot[s % 2], HOTS), over(C["count"], [P, HOTS, P], 1),
                   over(lo_f[:, turn], [P, HOTS, P], 2), ALU.is_equal).then_inc(lane_hot_ready, 1)
                if s == 1:
                    shared_multiply(0, 3)
            dve.wait_ge(slots_psum, HOT_TURNS)
            nc.vector.tensor_copy(slot_w[:, :], ps_slots[:, JW:2 * JW])
            nc.vector.tensor_copy(slot_token[:, :], ps_slots[:, 0:JW]).then_inc(slots_ready, 1)
            for t in range(GT):
                shared_add(0, t)
            dve.wait_ge(slots_ready, 1)

            def expert(h, b, n):
                j = 2 * h + b
                if n is None or 1 <= n <= SLOT_TILES:
                    dve.wait_ge(actT_psum, j)
                    wait(dve, down_psum, j - 2)
                    nc.vector.tensor_copy(actT_sb[1 - b], ps_actT[:, 0:P]).then_inc(actT_ready, 1)
                if n is None or n < SLOT_TILES:
                    dve.wait_ge(silu_ready, j + 1)
                    stt(act_sb[:, :], ps_gu[b][:, INTER:2 * INTER], slot_w[:, bass.ds(j, 1)], silu_sb[:, 0:INTER],
                        ALU.mult, ALU.mult).then_inc(act_ready, 1)
                if n is None or n >= 2:
                    dve.wait_ge(down_psum, j - 1)
                    wait(dve, y_stored[b], 16 * (h - 1))
                    nc.vector.tensor_copy(y_out[b], ps_y[b][:, :]).then_inc(y_ready, 1)

            for n in range(2):
                expert(0, n, n)
            with dve.Fori(1, SLOT_TILES // 2) as h:
                for b in range(2):
                    expert(h, b, None)
            expert(SLOT_TILES // 2, 0, SLOT_TILES - 1)

            def add_results(quad, u):
                t = quad * GT + u
                dst = tile_of(resid, t)
                for k in range(CHOICES):
                    buf = u * CHOICES + k
                    dve.wait_ge(y_gathered[buf], 16 * (quad + 1))
                    if k == 0:
                        tt(dst, dst, y_in[buf], ALU.add).then_inc(y_half_added, 1)
                        dve.wait_ge(y_half_added, t + 1)
                    else:
                        tt(dst, dst, y_in[buf], ALU.add).then_inc(y_added, 1)

            def rest(dst, src, hi, done, hi_ready, value):
                dve.wait_ge(hi_ready, value)
                tt(dst, src, hi.bitcast(F32), ALU.subtract).then_inc(done, 1)

            def weights_lo(first, last):
                for i in range(first, min(last, len(WEIGHT_BLOCKS))):
                    rest(*(weight_block(w, *WEIGHT_BLOCKS[i]) for w in (shgu_lo, shgu_sb, shgu_hi)),
                         weights_lo_ready, weights_hi_ready, i + 1)

            def down_weights_lo(m):
                rest(*(w[:, m * D:(m + 1) * D] for w in (shd_lo, shd_sb, shd_hi)),
                     weights_lo_ready, weights_hi_ready, len(WEIGHT_BLOCKS) + m + 1)

            def split_tokens_lo(g):
                for t in range(GT):
                    cols = slice(t * D, (t + 1) * D)
                    rest(tokens_halves[1][:, cols], tile_of(x2T, g * GT + t), tokens_halves[0][:, cols],
                         tokens_lo_ready, tokens_hi_ready, (g - 1) * GT + t + 1)

            def split_act_lo(g, m):
                cols = slice(m * D, (m + 1) * D)
                rest(by_tile(act_halves[1][:, cols]), act_block(m), by_tile(act_halves[0][:, cols]),
                     act_lo_ready, act_hi_ready, (g - 1) * SB + m + 1)

            split_tokens_lo(1)
            weights_lo(0, 1)
            expert(SLOT_TILES // 2, 1, SLOT_TILES)
            weights_lo(1, 2)
            expert(SLOT_TILES // 2 + 1, 0, SLOT_TILES + 1)
            weights_lo(2, 3)
            for m in range(SB):
                shared_multiply(1, m)
                weights_lo(3 + 2 * m, 5 + 2 * m)
                split_act_lo(1, m)
                if 1 <= m <= 2:
                    down_weights_lo(2 * m - 2)
                    down_weights_lo(2 * m - 1)
            split_tokens_lo(2)
            for t in range(GT):
                shared_add(1, t)
                add_results(0, t)
            for m in range(SB):
                shared_multiply(2, m)
                split_act_lo(2, m)
                add_results(1, m)
            split_tokens_lo(3)
            for t in range(GT):
                shared_add(2, t)
                dve.wait_ge(sh_added, 2 * GT + t + 1)
                add_results(2, t)
            for m in range(SB):
                shared_multiply(3, m)
                split_act_lo(3, m)
                add_results(3, m)
            dve.wait_ge(y_added, PAIRS)
            for t in range(GT):
                shared_add(3, t)

        @block.gpsimd
        def _(pool):
            def root(which, p):
                tt = nc.gpsimd.tensor_tensor
                pool.wait_ge(meanvar_ready[which], p + 1)
                wait(pool, (xn_ready, x2n_ready)[which], p)
                tt(negmean[which][:, :], meanvar[which][:, 0:1], C["minus_one"], ALU.mult)
                tt(veps[which][:, :], meanvar[which][:, 1:2], C["eps"], ALU.add).then_inc(veps_ready[which], 1)
                pool.wait_ge(veps_ready[which], p + 1)
                tt(rstd[which][:, :], veps[which][:, :], C["minus_half"], ALU.pow).then_inc(root_ready[which], 1)
                pool.wait_ge(root_ready[which], p + 1)
                tt(shift[which][:, :], negmean[which][:, :], rstd[which][:, :], ALU.mult).then_inc(rstd_ready[which], 1)

            def keep(h, b, n):
                if live(n, -3) and n != PAIRS + 2:
                    p, pb = pair(h, b, -3)
                    pool.wait_ge(x2T_ready, p + 1)
                    nc.gpsimd.tensor_copy(tile_of(x2T, p), x2T_tile[pb]).then_inc(x2T_kept, 1)

            def odd_product(h, b, n):
                if live(n, -1):
                    p, pb = pair(h, b, -1)
                    pool.wait_ge(w_odd_sw_ready, p + 1)
                    nc.gpsimd.tensor_tensor(w_odd_sw, w_odd_sw, ctx_odd_im[pb], ALU.mult).then_inc(odd_im_products, 1)
                    pool.wait_ge(out_products_ready, 2 * p + 2)
                    pool.wait_ge(odd_im_products, p + 1)
                    nc.gpsimd.tensor_tensor(odd_prod, odd_prod, w_odd_sw, ALU.add).then_inc(odd_product_ready, 1)

            def iteration(h, b, n):
                if live(n, -2):
                    p, _ = pair(h, b, -2)
                    root(1, p)
                if n == PAIRS:
                    odd_product(h, b, n)
                    keep(h, b, n)
                else:
                    keep(h, b, n)
                    if n != PAIRS - 1:
                        odd_product(h, b, n)
                if live(n, 0):
                    p, _ = pair(h, b, 0)
                    pool.wait_ge(masked, p + 1)
                    pool.wait_ge(top_r_ready, p + 1)
                    w = segs(lagw)
                    nc.gpsimd.tensor_tensor(w, w, top_r[:, :].unsqueeze(2).to_broadcast([P, SEGS, L]),
                                            ALU.mult).then_inc(lagw_ready, 1)
                if n == PAIRS - 1:
                    odd_product(h, b, n)
                if live(n, 2):
                    p, pb = pair(h, b, 2)
                    root(0, p)
                    if n != -2:
                        pool.wait_ge(ctx_hi_ready, p + 1)
                        nc.gpsimd.tensor_tensor(ctx_halves[1], ctx_in[pb], ctx_halves[0].bitcast(F32), ALU.subtract).then_inc(ctx_lo_ready, 1)

            pool.wait_ge(early_loaded, 16)
            run(pool, iteration)

            for s in range(HOT_TURNS):
                pool.wait_ge(tile_hot_found, s + 1)
                found, weighted = (by_choice(tile_hot[s % 2], 2 * HOTS)[:, v * HOTS:(v + 1) * HOTS] for v in range(2))
                first, dims = s * HOTS, [P, HOTS, JW]
                nc.gpsimd.tensor_tensor(weighted, found, r_w[:, first:first + HOTS].unsqueeze(2).to_broadcast(dims), ALU.mult)
                first %= PAIRS
                nc.gpsimd.tensor_tensor(found, found, C["token"][:, first:first + HOTS].unsqueeze(2).to_broadcast(dims),
                                        ALU.mult).then_inc(tile_hot_ready, 1)

            def gather(h, b):
                j = 2 * h + b
                wait(pool, gathered[b], 16 * h)
                nc.gpsimd.tensor_copy(gidx[b][:, :], slot_token[:, bass.ds(j, 1)]).then_inc(gidx_ready, 1)
                wait(pool, xgT_psum, j - 1)
                pool.wait_ge(gidx_ready, j + 1)
                apart(pool, pool_passed)
                nc.gpsimd.indirect_dma_start(xg[b], None, x2_rows[:, :],
                                             bass.IndirectOffsetOnAxis(ap=gidx[b][:, 0:1], axis=0)).then_inc(gathered[b], 16)

            pool.wait_ge(slots_ready, 1)
            for b in range(2):
                pool.wait_ge(x2_stored[b], 16 * PAIRS // 2)
                gather(0, b)
            with pool.Fori(1, SLOT_TILES // 2) as h:
                for b in range(2):
                    gather(h, b)
            gather(SLOT_TILES // 2, 0)

            pool.wait_ge(y_stored[0], 16 * ((SLOT_TILES + 1) // 2))
            pool.wait_ge(y_stored[1], 16 * (SLOT_TILES // 2))
            pool.wait_ge(pos_ready, 1)
            pool.wait_ge(gathered[0], 16 * ((SLOT_TILES + 1) // 2))
            pool.wait_ge(gathered[1], 16 * (SLOT_TILES // 2))
            pos = pos_i[:, :].rearrange("p (k t) -> p k t", k=CHOICES)

            def gather_results(turn, first=False):
                for buf in range(YBUFS):
                    u, k = buf // CHOICES, buf % CHOICES
                    t = turn * YTILES + u
                    wait(pool, y_gathered[buf], 16 * turn)
                    nc.gpsimd.tensor_copy(gidx[buf][:, :], pos[:, k, bass.ds(t, 1)]).then_inc(yidx_ready, 1)
                    pool.wait_ge(yidx_ready, turn * YBUFS + buf + 1)
                    if not first:
                        pool.wait_ge(y_added, t - YTILES + 1)
                    apart(pool, pool_passed)
                    nc.gpsimd.indirect_dma_start(y_in[buf], None, y_rows[:, :],
                                                 bass.IndirectOffsetOnAxis(ap=gidx[buf][:, 0:1], axis=0)).then_inc(y_gathered[buf], 16)

            gather_results(0, first=True)
            with pool.Fori(1, PAIRS * CHOICES // YBUFS) as turn:
                gather_results(turn)


def kernel(x, ctx_4096, L0_ffn_gate_w, L0_ffn_w_gate_up, L0_ffn_w_down, L0_ffn_shared_w_gate_up, L0_ffn_shared_w_down):
    import concourse.bacc as bacc
    from concourse.bass_utils import run_bass_kernel_spmd

    def blocks(w):
        w = np.asarray(w)
        return np.ascontiguousarray(w.reshape(w.shape[0], w.shape[1] // P, P).transpose(2, 1, 0)).reshape(P, -1)

    gu = np.asarray(L0_ffn_w_gate_up)
    arrays = {
        "x": np.ascontiguousarray(x).reshape(TOKENS, D),
        "ctx": np.ascontiguousarray(ctx_4096).reshape(TOKENS, D),
        "consts": constants(),
        "gate": blocks(L0_ffn_gate_w),
        "w_gu": np.ascontiguousarray(gu.reshape(E, 2 * INTER, KB, P).transpose(3, 0, 2, 1)).reshape(P, -1),
        "w_down": np.ascontiguousarray(np.asarray(L0_ffn_w_down).transpose(2, 0, 1)).reshape(P, -1),
        "sh_gu": blocks(L0_ffn_shared_w_gate_up),
        "sh_down": blocks(L0_ffn_shared_w_down),
    }
    nc = bacc.Bacc("TRN2", target_bir_lowering=False, num_devices=1)
    args = [nc.dram_tensor(n, a.shape, F32, kind="ExternalInput").ap() for n, a in arrays.items()]
    out = nc.dram_tensor("result", (TOKENS, D), F32, kind="ExternalOutput").ap()
    build(nc, *args, out)
    result = run_bass_kernel_spmd(nc, [arrays], core_ids=[0]).results[0]["result"]
    return result.reshape(SEQS, L, D)
```
